# Optimizing a Trainium2 kernel written in Bass

```python
import numpy as np
import jax
import jax.numpy as jnp

def _softmax(x, axis=-1):
    return jax.nn.softmax(x, axis=axis)
def _gelu(x):
    return jax.nn.gelu(x, approximate=True)
def _silu(x):
    return jax.nn.silu(x)
def _sigmoid(x):
    return jax.nn.sigmoid(x)
def _layernorm(x, axis=-1, eps=1e-5):
    m = jnp.mean(x, axis=axis, keepdims=True)
    v = jnp.var(x, axis=axis, keepdims=True)
    return (x - m) / jnp.sqrt(v + eps)
def _scatter_add(tgt, idx, src, axis=0):
    return tgt.at[idx].add(src)
def _segment_sum(src, seg, n):
    return jax.ops.segment_sum(src, seg, n)

kernel_name = 'mk_conv_preact_d4_conv_nchw32_3b920a'

def setup_inputs(seed: int = 0):
    np.random.seed(seed)
    _w = jnp.asarray
    def _rec_inputs():
        import jax
        import jax.numpy as jnp
        _gk = jax.random.key(seed)
        x = -0.0001329 + 0.9999 * jax.random.normal(jax.random.fold_in(_gk, 1), (8, 32, 384, 384), jnp.float32)
        return x
    x = _rec_inputs()
    def _L0_conv_setup():
        import jax, jax.numpy as jnp
        import numpy as np
        from jax import lax
        B, C, H, W = (16, 32, 384, 384)
        NK = 32
        K = 3
        HID = 128
        key = jax.random.key(seed)
        ks = jax.random.split(key, 5)
        x = jax.random.normal(ks[0], (B, C, H, W), dtype=jnp.float32)
        w1 = jax.random.normal(ks[1], (C, HID), dtype=jnp.float32) * (1.0 / np.sqrt(C))
        b1 = jnp.zeros((HID,), dtype=jnp.float32)
        w2 = jax.random.normal(ks[2], (HID, NK * K * K), dtype=jnp.float32) * (1.0 / np.sqrt(HID))
        b2 = jnp.zeros((NK * K * K,), dtype=jnp.float32)
        return {'x': x, 'w1': w1, 'b1': b1, 'w2': w2, 'b2': b2}
    _L0_conv_all = _L0_conv_setup()
    _L0_conv_in = {k: v for k, v in _L0_conv_all.items() if k in ('w1', 'b1', 'w2', 'b2', )}
    del _L0_conv_all

    def _L1_conv_setup():
        import jax, jax.numpy as jnp
        import numpy as np
        from jax import lax
        B, C, H, W = (16, 32, 384, 384)
        NK = 32
        K = 3
        HID = 128
        key = jax.random.key(seed)
        ks = jax.random.split(key, 5)
        x = jax.random.normal(ks[0], (B, C, H, W), dtype=jnp.float32)
        w1 = jax.random.normal(ks[1], (C, HID), dtype=jnp.float32) * (1.0 / np.sqrt(C))
        b1 = jnp.zeros((HID,), dtype=jnp.float32)
        w2 = jax.random.normal(ks[2], (HID, NK * K * K), dtype=jnp.float32) * (1.0 / np.sqrt(HID))
        b2 = jnp.zeros((NK * K * K,), dtype=jnp.float32)
        return {'x': x, 'w1': w1, 'b1': b1, 'w2': w2, 'b2': b2}
    _L1_conv_all = _L1_conv_setup()
    _L1_conv_in = {k: v for k, v in _L1_conv_all.items() if k in ('w1', 'b1', 'w2', 'b2', )}
    del _L1_conv_all

    def _L2_conv_setup():
        import jax, jax.numpy as jnp
        import numpy as np
        B, C, H, W = (8, 32, 384, 384)
        PLANES, K, P, D, OFFSET = (32, 3, 1, 1, 1)

        def conv2d(x, w, b, pad, dil=1):
            out = jax.lax.conv_general_dilated(x, w, window_strides=(1, 1), padding=[(pad, pad), (pad, pad)], rhs_dilation=(dil, dil), dimension_numbers=('NCHW', 'OIHW', 'NCHW'))
            return out + b[None, :, None, None]

        def reflect(t, rng):
            two = 2.0 * rng
            m = jnp.mod(jnp.abs(t), two)
            r = jnp.where(m > rng, two - m, m)
            return jnp.clip(r, 0.0, rng)
        key = jax.random.key(seed)
        k1, k2, k3 = jax.random.split(key, 3)
        x = jax.random.normal(k1, (B, C, H, W), dtype=jnp.float32)
        koff = 2 * OFFSET + 1
        w_off = jax.random.normal(k2, (2 * C, C, koff, koff), dtype=jnp.float32) * (1.0 / np.sqrt(C * koff * koff))
        b_off = jnp.zeros((2 * C,), dtype=jnp.float32)
        w_dcn = jax.random.normal(k3, (PLANES, C, K, K), dtype=jnp.float32) * (1.0 / np.sqrt(C * K * K))
        b_dcn = jnp.zeros((PLANES,), dtype=jnp.float32)
        return {'x': x, 'w_off': w_off, 'b_off': b_off, 'w_dcn': w_dcn, 'b_dcn': b_dcn}
    _L2_conv_all = _L2_conv_setup()
    _L2_conv_in = {k: v for k, v in _L2_conv_all.items() if k in ('w_off', 'b_off', 'w_dcn', 'b_dcn', )}
    del _L2_conv_all

    def _L3_conv_setup():
        import jax, jax.numpy as jnp
        import numpy as np
        from jax import lax
        B, C, H, W = (16, 32, 384, 384)
        NK = 32
        K = 3
        HID = 128
        key = jax.random.key(seed)
        ks = jax.random.split(key, 5)
        x = jax.random.normal(ks[0], (B, C, H, W), dtype=jnp.float32)
        w1 = jax.random.normal(ks[1], (C, HID), dtype=jnp.float32) * (1.0 / np.sqrt(C))
        b1 = jnp.zeros((HID,), dtype=jnp.float32)
        w2 = jax.random.normal(ks[2], (HID, NK * K * K), dtype=jnp.float32) * (1.0 / np.sqrt(HID))
        b2 = jnp.zeros((NK * K * K,), dtype=jnp.float32)
        return {'x': x, 'w1': w1, 'b1': b1, 'w2': w2, 'b2': b2}
    _L3_conv_all = _L3_conv_setup()
    _L3_conv_in = {k: v for k, v in _L3_conv_all.items() if k in ('w1', 'b1', 'w2', 'b2', )}
    del _L3_conv_all

    return {
        "x": x,
        "L0_conv_w1": _L0_conv_in["w1"],
        "L0_conv_b1": _L0_conv_in["b1"],
        "L0_conv_w2": _L0_conv_in["w2"],
        "L0_conv_b2": _L0_conv_in["b2"],
        "L1_conv_w1": _L1_conv_in["w1"],
        "L1_conv_b1": _L1_conv_in["b1"],
        "L1_conv_w2": _L1_conv_in["w2"],
        "L1_conv_b2": _L1_conv_in["b2"],
        "L2_conv_w_off": _L2_conv_in["w_off"],
        "L2_conv_b_off": _L2_conv_in["b_off"],
        "L2_conv_w_dcn": _L2_conv_in["w_dcn"],
        "L2_conv_b_dcn": _L2_conv_in["b_dcn"],
        "L3_conv_w1": _L3_conv_in["w1"],
        "L3_conv_b1": _L3_conv_in["b1"],
        "L3_conv_w2": _L3_conv_in["w2"],
        "L3_conv_b2": _L3_conv_in["b2"],
    }

def reference(x, L0_conv_w1, L0_conv_b1, L0_conv_w2, L0_conv_b2, L1_conv_w1, L1_conv_b1, L1_conv_w2, L1_conv_b2, L2_conv_w_off, L2_conv_b_off, L2_conv_w_dcn, L2_conv_b_dcn, L3_conv_w1, L3_conv_b1, L3_conv_w2, L3_conv_b2):
    import jax
    import jax.numpy as jnp
    def _L0_conv_ref(x, w1, b1, w2, b2):
        import jax, jax.numpy as jnp
        import numpy as np
        from jax import lax
        B, C, H, W = (16, 32, 384, 384)
        NK = 32
        K = 3
        HID = 128
        b, c, h, w = x.shape
        pooled = x.mean(axis=(2, 3))
        hdn = jax.nn.relu(pooled @ w1 + b1)
        kernels = (hdn @ w2 + b2).reshape(b, NK, K, K)
        xg = x[:, :NK].reshape(1, b * NK, h, w)
        wgt = kernels.reshape(b * NK, 1, K, K)
        pad = K // 2
        out = lax.conv_general_dilated(xg, wgt, window_strides=(1, 1), padding=[(pad, pad), (pad, pad)], feature_group_count=b * NK, dimension_numbers=('NCHW', 'OIHW', 'NCHW'))
        return out.reshape(b, NK, h, w)

    def _L1_conv_ref(x, w1, b1, w2, b2):
        import jax, jax.numpy as jnp
        import numpy as np
        from jax import lax
        B, C, H, W = (16, 32, 384, 384)
        NK = 32
        K = 3
        HID = 128
        b, c, h, w = x.shape
        pooled = x.mean(axis=(2, 3))
        hdn = jax.nn.relu(pooled @ w1 + b1)
        kernels = (hdn @ w2 + b2).reshape(b, NK, K, K)
        xg = x[:, :NK].reshape(1, b * NK, h, w)
        wgt = kernels.reshape(b * NK, 1, K, K)
        pad = K // 2
        out = lax.conv_general_dilated(xg, wgt, window_strides=(1, 1), padding=[(pad, pad), (pad, pad)], feature_group_count=b * NK, dimension_numbers=('NCHW', 'OIHW', 'NCHW'))
        return out.reshape(b, NK, h, w)

    def _L2_conv_ref(x, w_off, b_off, w_dcn, b_dcn):
        import jax, jax.numpy as jnp
        import numpy as np
        B, C, H, W = (8, 32, 384, 384)
        PLANES, K, P, D, OFFSET = (32, 3, 1, 1, 1)

        def conv2d(x, w, b, pad, dil=1):
            out = jax.lax.conv_general_dilated(x, w, window_strides=(1, 1), padding=[(pad, pad), (pad, pad)], rhs_dilation=(dil, dil), dimension_numbers=('NCHW', 'OIHW', 'NCHW'))
            return out + b[None, :, None, None]

        def reflect(t, rng):
            two = 2.0 * rng
            m = jnp.mod(jnp.abs(t), two)
            r = jnp.where(m > rng, two - m, m)
            return jnp.clip(r, 0.0, rng)
        b, c, h, w = x.shape
        n = b * c
        off = (jax.nn.sigmoid(conv2d(x, w_off, b_off, OFFSET * D, D)) - 0.5) * (2.0 * OFFSET)
        off = off.reshape(n, 2, h, w)
        offx = off[:, 0] / (w - 1)
        offy = off[:, 1] / (h - 1)
        gy_base = jnp.arange(h, dtype=jnp.float32) / (h - 1) * 2.0 - 1.0
        gx_base = jnp.arange(w, dtype=jnp.float32) / (w - 1) * 2.0 - 1.0
        gx = gx_base[None, None, :] - offx
        gy = gy_base[None, :, None] - offy
        ix = reflect((gx + 1.0) * 0.5 * (w - 1), float(w - 1))
        iy = reflect((gy + 1.0) * 0.5 * (h - 1), float(h - 1))
        ix0 = jnp.floor(ix)
        iy0 = jnp.floor(iy)
        wx = ix - ix0
        wy = iy - iy0
        i0 = jnp.clip(ix0, 0, w - 1).astype(jnp.int32)
        i1 = jnp.clip(ix0 + 1, 0, w - 1).astype(jnp.int32)
        j0 = jnp.clip(iy0, 0, h - 1).astype(jnp.int32)
        j1 = jnp.clip(iy0 + 1, 0, h - 1).astype(jnp.int32)
        planes = x.reshape(n, h, w)
        nidx = jnp.arange(n)[:, None, None]
        v00 = planes[nidx, j0, i0]
        v01 = planes[nidx, j0, i1]
        v10 = planes[nidx, j1, i0]
        v11 = planes[nidx, j1, i1]
        sampled = v00 * (1 - wy) * (1 - wx) + v01 * (1 - wy) * wx + v10 * wy * (1 - wx) + v11 * wy * wx
        out = sampled.reshape(b, c, h, w)
        return conv2d(out, w_dcn, b_dcn, P, D)

    def _L3_conv_ref(x, w1, b1, w2, b2):
        import jax, jax.numpy as jnp
        import numpy as np
        from jax import lax
        B, C, H, W = (16, 32, 384, 384)
        NK = 32
        K = 3
        HID = 128
        b, c, h, w = x.shape
        pooled = x.mean(axis=(2, 3))
        hdn = jax.nn.relu(pooled @ w1 + b1)
        kernels = (hdn @ w2 + b2).reshape(b, NK, K, K)
        xg = x[:, :NK].reshape(1, b * NK, h, w)
        wgt = kernels.reshape(b * NK, 1, K, K)
        pad = K // 2
        out = lax.conv_general_dilated(xg, wgt, window_strides=(1, 1), padding=[(pad, pad), (pad, pad)], feature_group_count=b * NK, dimension_numbers=('NCHW', 'OIHW', 'NCHW'))
        return out.reshape(b, NK, h, w)

    def _gn(v, G=16, eps=1e-5):
        B_, C_, H_, W_ = v.shape
        g = v.reshape(B_, G, C_ // G, H_, W_)
        m = jnp.mean(g, axis=(2, 3, 4), keepdims=True)
        s = jnp.var(g, axis=(2, 3, 4), keepdims=True)
        return ((g - m) / jnp.sqrt(s + eps)).reshape(v.shape)

    def _ln_c(v, eps=1e-6):
        m = jnp.mean(v, axis=1, keepdims=True)
        s = jnp.var(v, axis=1, keepdims=True)
        return (v - m) / jnp.sqrt(s + eps)

    def _ln_t(v, eps=1e-5):
        m = jnp.mean(v, axis=-1, keepdims=True)
        s = jnp.var(v, axis=-1, keepdims=True)
        return (v - m) / jnp.sqrt(s + eps)

    def _to_tokens(v):
        B_, C_, H_, W_ = v.shape
        return v.reshape(B_, C_, H_ * W_).transpose(0, 2, 1)
    def _from_tokens(t, like):
        B_, C_, H_, W_ = like.shape
        return t.transpose(0, 2, 1).reshape(B_, C_, H_, W_)

    x = x + _L0_conv_ref(_gn(x), L0_conv_w1, L0_conv_b1, L0_conv_w2, L0_conv_b2)
    x = x + _L1_conv_ref(_gn(x), L1_conv_w1, L1_conv_b1, L1_conv_w2, L1_conv_b2)
    x = x + _L2_conv_ref(_gn(x), L2_conv_w_off, L2_conv_b_off, L2_conv_w_dcn, L2_conv_b_dcn)
    x = x + _L3_conv_ref(_gn(x), L3_conv_w1, L3_conv_b1, L3_conv_w2, L3_conv_b2)
    return x


_drawn_inputs = setup_inputs


def setup_inputs(seed=0):
    import zlib

    import numpy as np

    out = dict(_drawn_inputs(seed))
    spreads = {'L0_conv_b1': (0.0, 0.1),
     'L0_conv_b2': (0.0, 0.1),
     'L1_conv_b1': (0.0, 0.1),
     'L1_conv_b2': (0.0, 0.1),
     'L2_conv_b_off': (0.0, 0.316),
     'L2_conv_b_dcn': (0.0, 0.1),
     'L3_conv_b1': (0.0, 0.1),
     'L3_conv_b2': (0.0, 0.1)}
    factors = {'L0_conv_w1': 8.0, 'L1_conv_w1': 8.0}
    for name, (base, spread) in spreads.items():
        noise = np.random.default_rng([zlib.crc32(name.encode()), seed]).standard_normal(out[name].shape)
        drawn = base * np.exp(spread * noise) if base else spread * noise
        out[name] = jnp.asarray(drawn.astype(out[name].dtype))
    for name, factor in factors.items():
        out[name] = (out[name] * factor).astype(out[name].dtype)
    return out
```

```python
from contextlib import ExitStack

import concourse.bass as bass
from concourse import mybir

F32 = mybir.dt.float32
ALU = mybir.AluOpType
ACT = mybir.ActivationFunctionType
AX_X = mybir.AxisListType.X
ds = bass.ds

B, C, H, W = 8, 32, 384, 384
NQ = B * C
HW = H * W
HID = 128
TAPS = 9
EPS = 1e-5
TR = 96
NT = H // TR
KR = TR + 2
WP = W + 2
GC = 4
HALF = W // 2
PARTS = HW // HALF
NCH = 12
CS = 4
NST = NCH * CS
STRIPS = NST + 1
FR = 2 * CS + 2


class Memory:
    pass


def setup(nc, m, w):
    with nc.semaphore("zeroed") as zeroed, nc.semaphore("weights_loaded") as loaded, \
            nc.semaphore("masks_done") as masks, nc.semaphore("halved") as halved, nc.Block() as block:

        @block.vector
        def _(dve):
            nc.vector.memset(m.w_off[:], 0.0)
            nc.vector.memset(m.w_dcn[:], 0.0)
            nc.vector.memset(m.ones[:], 1.0)
            nc.vector.memset(m.band[:], 0.0)
            nc.vector.memset(m.sel[:], 0.0)
            nc.vector.memset(m.row_mask[:], 1.0).then_inc(zeroed, 1)
            dve.wait_ge(loaded, 16 * len(w.loads))
            nc.vector.tensor_scalar(m.half_b_off[:], m.half_b_off[:], 0.5, None, ALU.mult).then_inc(halved, 1)

        @block.sync
        def _(sp):
            sp.wait_ge(zeroed, 1)
            for dst, src in w.loads:
                sp.dma_start(dst, src).then_inc(loaded, 16)
            sp.wait_ge(loaded, 16 * len(w.loads))

        @block.gpsimd
        def _(pool):
            pool.wait_ge(zeroed, 1)
            for dy in range(3):
                nc.gpsimd.affine_select(out=m.band[:, dy, :], in_=m.band[:, dy, :], compare_op=ALU.not_equal,
                                        fill=1.0, base=-dy, pattern=[[-1, TR]],
                                        channel_multiplier=1).then_inc(masks, 1)
            for b in range(4):
                pool.wait_ge(masks, 3 + b)
                nc.gpsimd.affine_select(out=m.sel[:], in_=m.sel[:], compare_op=ALU.not_equal, fill=1.0,
                                        base=-C * b, pattern=[[-1, C]], channel_multiplier=1).then_inc(masks, 1)
            nc.gpsimd.affine_select(out=m.row_mask[:, 0:1], in_=m.row_mask[:, 0:1], compare_op=ALU.not_equal,
                                    fill=0.0, base=0, pattern=[[0, 1]], channel_multiplier=1).then_inc(masks, 1)
            nc.gpsimd.affine_select(out=m.row_mask[:, 2:3], in_=m.row_mask[:, 2:3], compare_op=ALU.not_equal,
                                    fill=0.0, base=-(KR - 1), pattern=[[0, 1]], channel_multiplier=1).then_inc(masks, 1)
            pool.wait_ge(masks, 9)


def input_statistics(nc, m, x):
    src = x.rearrange("b c (p r) w -> p (b c) (r w)", p=TR)
    with nc.sbuf_tensor("xin", [TR, 2, GC, NT * W], F32) as xin, nc.semaphore("stat_load0") as load0, \
            nc.semaphore("stat_load1") as load1, nc.semaphore("stat_done") as done, nc.Block() as block:
        loaded = [load0, load1]

        @block.sync
        def _(sp):
            with sp.Fori(0, NQ // (2 * GC)) as it:
                for sl in range(2):
                    sp.wait_ge(done, it * 2 + sl + 1)
                    sp.dma_start(xin[:, sl], src[:, ds((it * 2 + sl) * GC, GC)]).then_inc(loaded[sl], 16)

        @block.vector
        def _(dve):
            nc.vector.memset(m.scratch[:, 0:1], 0.0).then_inc(done, 2)
            with dve.Fori(0, NQ // (2 * GC)) as it:
                for sl in range(2):
                    dve.wait_ge(loaded[sl], it * 16 + 16)
                    for j in range(GC):
                        for t in range(NT):
                            ins = nc.vector.bn_stats(
                                m.stat[0:TR, ds((it * 2 + sl) * GC + j, 1), t].rearrange("p a k -> p (a k)"),
                                xin[:, sl, j, t * W:(t + 1) * W])
                    ins.then_inc(done, 1)


def parameters(nc, m, layer, from_blocks, net):
    with ExitStack() as ctx:
        def sem(name):
            return ctx.enter_context(nc.semaphore(f"{name}_{layer}"))

        means_summed, sums = sem("means_summed"), sem("sums")
        vars_summed, var_sums = sem("vars_summed"), sem("var_sums")
        var_ready, sqrt_done = sem("var_ready"), sem("sqrt_done")
        pooled_ready, hidden_sums = sem("pooled_ready"), sem("hidden_sums")
        hidden_ready, kernel_sums = sem("hidden_ready"), sem("kernel_sums")
        step = sem("parameter_step")
        block = ctx.enter_context(nc.Block())
        rows = 4 * C if from_blocks else TR
        if from_blocks:
            part = m.stat2[:].rearrange("p s r (e k) -> p s (r e) k", k=3)
        else:
            part = m.stat[0:TR].rearrange("p q t (e k) -> p q (t e) k", k=3)
        n_col, n_part = part.shape[1], part.shape[2]
        diff = m.scratch[0:rows, 0:n_col * n_part].rearrange("p (q t) -> p q t", t=n_part)

        @block.vector
        def _(dve):
            done = [0]

            def link(ins):
                done[0] += 1
                ins.then_inc(step, 1)
                dve.wait_ge(step, done[0])

            def spread(dst, col):
                nc.vector.tensor_tensor(
                    dst.rearrange("p (s c) -> p s c", c=C), col.unsqueeze(2).broadcast_to([4 * C, B, C]),
                    m.sel[:].unsqueeze(1).broadcast_to([4 * C, B, C]), ALU.mult).then_inc(step, 1)
                done[0] += 1
                dve.wait_ge(step, done[0])

            def column(dst, row):
                tmp = m.scratch[:, 0:NQ].rearrange("p (s c) -> p s c", c=C)
                link(nc.vector.tensor_tensor(tmp, row.rearrange("p (s c) -> p s c", c=C),
                                             m.sel[:].unsqueeze(1).broadcast_to([4 * C, B, C]), ALU.mult))
                link(nc.vector.tensor_reduce(dst, tmp, AX_X, ALU.add))

            link(nc.vector.tensor_reduce(m.col_sum[0:rows, 0:n_col], part[:, :, :, 1], AX_X, ALU.add))
            if from_blocks:
                spread(m.row_sum[:], m.col_sum[:, 0:B])
            else:
                link(nc.vector.tensor_copy(m.row_sum[0:TR, :], m.col_sum[0:TR, :]))
            nc.vector.memset(m.scratch[:, 0:1], 0.0).then_inc(means_summed, 1)
            dve.wait_ge(sums, 1)
            link(nc.vector.tensor_scalar(m.chan_mean[:], m.ps[:, 0, 0:NQ], 1.0 / PARTS, None, ALU.mult))
            pair = m.chan_mean[:].rearrange("p (g e) -> p g e", e=2)
            link(nc.vector.tensor_tensor(m.pair[:], pair[:, :, 0], pair[:, :, 1], ALU.add))
            link(nc.vector.tensor_scalar(m.mean[:].rearrange("p (g e) -> p g e", e=2),
                                         m.pair[:].unsqueeze(2).broadcast_to([128, NQ // 2, 2]),
                                         0.5, None, ALU.mult))
            if from_blocks:
                column(m.mean_col[:], m.mean[:])
                middle = m.mean_col[:]
            else:
                middle = m.mean[0:TR, :]
            link(nc.vector.tensor_tensor(diff, part[:, :, :, 1],
                                         middle.unsqueeze(2).broadcast_to([rows, n_col, n_part]), ALU.subtract))
            link(nc.vector.tensor_tensor(diff, diff, diff, ALU.mult))
            link(nc.vector.scalar_tensor_tensor(out=diff, in0=diff, scalar=float(HALF), in1=part[:, :, :, 2],
                                                op0=ALU.mult, op1=ALU.add))
            link(nc.vector.tensor_reduce(m.col_sum[0:rows, 0:n_col], diff, AX_X, ALU.add))
            if from_blocks:
                spread(m.row_sum[:], m.col_sum[:, 0:B])
            else:
                link(nc.vector.tensor_copy(m.row_sum[0:TR, :], m.col_sum[0:TR, :]))
            nc.vector.memset(m.scratch[:, 0:1], 0.0).then_inc(vars_summed, 1)
            dve.wait_ge(var_sums, 1)
            link(nc.vector.tensor_copy(m.chan_var[:], m.ps[:, 1, 0:NQ]))
            pair = m.chan_var[:].rearrange("p (g e) -> p g e", e=2)
            link(nc.vector.tensor_tensor(m.pair[:], pair[:, :, 0], pair[:, :, 1], ALU.add))
            link(nc.vector.tensor_scalar(m.pair[:], m.pair[:], 1.0 / (2 * HW), EPS, ALU.mult, ALU.add))
            nc.vector.memset(m.scratch[:, 0:1], 0.0).then_inc(var_ready, 1)
            dve.wait_ge(sqrt_done, 1)
            link(nc.vector.reciprocal(m.rough[:], m.root[:]))
            link(nc.vector.tensor_tensor(m.root[:], m.rough[:], m.rough[:], ALU.mult))
            link(nc.vector.tensor_tensor(m.root[:], m.root[:], m.pair[:], ALU.mult))
            link(nc.vector.tensor_scalar(m.root[:], m.root[:], -0.5, 1.5, ALU.mult, ALU.add))
            link(nc.vector.tensor_tensor(m.rough[:], m.rough[:], m.root[:], ALU.mult))
            link(nc.vector.tensor_copy(m.rstd[:].rearrange("p (g e) -> p g e", e=2),
                                       m.rough[:].unsqueeze(2).broadcast_to([128, NQ // 2, 2])))
            if net is None:
                column(m.mean_col[:], m.mean[:])
                column(m.rstd_col[:], m.rstd[:])
                link(nc.vector.reciprocal(m.std_col[:], m.rstd_col[:]))
                link(nc.vector.tensor_tensor(m.shift_col[:], m.mean_col[:], m.rstd_col[:], ALU.mult))
                link(nc.vector.tensor_scalar(m.shift_col[:], m.shift_col[:], -1.0, None, ALU.mult))
                link(nc.vector.tensor_scalar(m.out_bias[:], m.mean_col[:], m.b_dcn[:, 0:1], None, ALU.add))
                return
            for k in range(3):
                link(nc.vector.tensor_scalar(m.row_mean[:, k], m.mean[:], m.row_mask[:, k:k + 1], None, ALU.mult))
            link(nc.vector.tensor_tensor(m.chan_mean[:], m.chan_mean[:], m.mean[:], ALU.subtract))
            link(nc.vector.tensor_tensor(m.chan_mean[:], m.chan_mean[:], m.rstd[:], ALU.mult))
            column(m.pooled[:], m.chan_mean[:])
            nc.vector.memset(m.scratch[:, 0:1], 0.0).then_inc(pooled_ready, 1)
            dve.wait_ge(hidden_sums, 1)
            link(nc.vector.tensor_scalar(m.hidden[:], m.ps[:, 2, 0:B], net.b1[:, 0:1], 0.0, ALU.add, ALU.max))
            nc.vector.tensor_copy(m.hidden_wide[:], m.hidden[:].unsqueeze(2).broadcast_to([HID, B, 128])) \
                .then_inc(hidden_ready, 1)
            dve.wait_ge(kernel_sums, 1)
            kern = m.kern[:].rearrange("p (s c) k -> p s (c k)", s=B)
            link(nc.vector.tensor_tensor(kern, m.ps[:, :, 0:C * TAPS],
                                         net.b2[:].unsqueeze(1).broadcast_to([128, B, C * TAPS]), ALU.add))
            link(nc.vector.tensor_tensor(m.kern[:], m.kern[:],
                                         m.rstd[:].unsqueeze(2).broadcast_to([128, NQ, TAPS]), ALU.mult))
            link(nc.vector.tensor_scalar(m.kern[:, :, TAPS // 2], m.kern[:, :, TAPS // 2], 1.0, None, ALU.add))

        @block.tensor
        def _(pe):
            pe.wait_ge(means_summed, 1)
            nc.tensor.matmul(m.ps[:, 0, 0:NQ], m.ones[0:rows, :], m.row_sum[0:rows, :], start=True, stop=True) \
                .then_inc(sums, 1)
            pe.wait_ge(vars_summed, 1)
            nc.tensor.matmul(m.ps[:, 1, 0:NQ], m.ones[0:rows, :], m.row_sum[0:rows, :], start=True, stop=True) \
                .then_inc(var_sums, 1)
            if net is None:
                return
            pe.wait_ge(pooled_ready, 1)
            nc.tensor.matmul(m.ps[:, 2, 0:B], net.w1[:, :], m.pooled[0:C, :], start=True, stop=True) \
                .then_inc(hidden_sums, 1)
            pe.wait_ge(hidden_ready, 1)
            for s in range(B):
                ins = nc.tensor.matmul(m.ps[:, s, 0:C * TAPS], m.hidden_wide[:, s, :], net.w2[:, :],
                                       start=True, stop=True)
            ins.then_inc(kernel_sums, 1)

        @block.scalar
        def _(act):
            act.wait_ge(var_ready, 1)
            nc.scalar.activation(m.root[:], m.pair[:], ACT.Sqrt).then_inc(sqrt_done, 1)


def depthwise(nc, m, layer, src, dst, statistics):
    xs = src.rearrange("b c h w -> h (b c) w")
    ys = dst.rearrange("b c (t p) w -> p (b c) t w", p=TR)
    with ExitStack() as ctx:
        def sem(name):
            return ctx.enter_context(nc.semaphore(f"{name}_{layer}"))

        def sb(name, shape):
            return ctx.enter_context(nc.sbuf_tensor(f"{name}_{layer}", shape, F32))

        xt = sb("x_tiles", [KR, 2, GC, NT, WP])
        yt = sb("y_tiles", [TR, 2, GC, NT, W])
        mat = sb("banded", [KR, 4, 3, TR])
        term = sb("banded_terms", [KR, 2, 3, TR])
        pads_zero = sem("pads_zero")
        loaded = [sem("x_loaded0"), sem("x_loaded1")]
        stored = [sem("y_stored0"), sem("y_stored1")]
        centred = sem("centred")
        built = sem("matrices_built")
        build_step = sem("build_step")
        conv_done = sem("conv_done")
        evacuated = sem("evacuated")
        stat_done = sem("stat_done")
        block = ctx.enter_context(nc.Block())
        NG = NQ // (2 * GC)

        @block.sync
        def _(sp):
            sp.wait_ge(pads_zero, 3)
            with sp.Fori(0, NG) as it:
                for sl in range(2):
                    q0 = (it * 2 + sl) * GC
                    sp.wait_ge(conv_done, q0 + 4)
                    for t in range(NT):
                        lo, hi = max(t * TR - 1, 0), min(t * TR + TR + 1, H)
                        p0 = lo - (t * TR - 1)
                        sp.dma_start(xt[p0:p0 + hi - lo, sl, :, t, 1:W + 1], xs[lo:hi, ds(q0, GC)]) \
                            .then_inc(loaded[sl], 16)

        @block.gpsimd
        def _(pool):
            with pool.Fori(0, NG) as it:
                for j in range(2 * GC):
                    q = it * (2 * GC) + j

                    def tap(dy):
                        return m.kern[0:KR, ds(q, 1), 3 * dy:3 * dy + 3].rearrange("p a k -> p (a k)") \
                            .unsqueeze(2).broadcast_to([KR, 3, TR])

                    def band(dy):
                        return m.band[0:KR, dy, :].unsqueeze(1).broadcast_to([KR, 3, TR])

                    pool.wait_ge(conv_done, q + 5)
                    nc.gpsimd.tensor_tensor(mat[:, j % 4], band(0), tap(0), ALU.mult)
                    nc.gpsimd.tensor_tensor(term[:, 0], band(1), tap(1), ALU.mult)
                    nc.gpsimd.tensor_tensor(term[:, 1], band(2), tap(2), ALU.mult).then_inc(build_step, 1)
                    pool.wait_ge(build_step, q * 2 + 1)
                    nc.gpsimd.tensor_tensor(mat[:, j % 4], mat[:, j % 4], term[:, 0], ALU.add) \
                        .then_inc(build_step, 1)
                    pool.wait_ge(build_step, q * 2 + 2)
                    nc.gpsimd.tensor_tensor(mat[:, j % 4], mat[:, j % 4], term[:, 1], ALU.add).then_inc(built, 1)
                    pool.wait_ge(built, q + 1)

        @block.tensor
        def _(pe):
            with pe.Fori(0, NG) as it:
                for j in range(2 * GC):
                    q = it * (2 * GC) + j
                    pe.wait_ge(centred, q + 1)
                    pe.wait_ge(built, q + 1)
                    pe.wait_ge(evacuated, q + 1)
                    for dx in range(3):
                        for t in range(NT):
                            ins = nc.tensor.matmul(m.ps[0:TR, 4 * (j % 2) + t, 0:W], mat[:, j % 4, dx, :],
                                                   xt[:, j // GC, j % GC, t, dx:dx + W],
                                                   start=(dx == 0), stop=(dx == 2))
                    ins.then_inc(conv_done, 1)

        @block.scalar
        def _(act):
            with act.Fori(0, NG) as it:
                for j in range(2 * GC):
                    q = it * (2 * GC) + j
                    sl = j // GC
                    if j % GC == 0:
                        act.wait_ge(stored[sl], it * 64 + 16)
                        if statistics:
                            act.wait_ge(stat_done, q + 4)
                    act.wait_ge(conv_done, q + 9)
                    act.wait_ge(pads_zero, 3)
                    nc.scalar.activation(yt[:, sl, j % GC], m.ps[0:TR, 4 * (j % 2):4 * (j % 2) + 4, 0:W],
                                         ACT.Identity, bias=m.mean[0:TR, ds(q, 1)]).then_inc(evacuated, 1)
                    act.wait_ge(evacuated, q + 3)
                    act.dma_start(ys[:, ds(q, 1)].rearrange("p a t w -> p (a t) w"), yt[:, sl, j % GC]) \
                        .then_inc(stored[sl], 16)
            for sl in range(2):
                act.wait_ge(stored[sl], NG * 64 + 16)

        @block.vector
        def _(dve):
            nc.vector.memset(xt[:, :, :, :, 0:WP:WP - 1].rearrange("p a b c d -> p (a b c) d"), 0.0) \
                .then_inc(pads_zero, 1)
            dve.wait_ge(pads_zero, 1)
            nc.vector.memset(xt[0:1, :, :, 0, :].rearrange("p a b d -> p (a b) d"), 0.0).then_inc(pads_zero, 1)
            dve.wait_ge(pads_zero, 2)
            nc.vector.memset(xt[TR:KR, :, :, NT - 1, :].rearrange("p a b d -> p (a b) d"), 0.0) \
                .then_inc(pads_zero, 1)
            nc.vector.memset(m.scratch[:, 0:1], 0.0).then_inc(conv_done, 8)
            nc.vector.memset(m.scratch[:, 1:2], 0.0).then_inc(evacuated, 2)
            nc.vector.memset(m.scratch[:, 2:3], 0.0).then_inc(stat_done, 8)
            nc.vector.memset(m.scratch[:, 3:4], 0.0).then_inc(stored[0], 16)
            nc.vector.memset(m.scratch[:, 4:5], 0.0).then_inc(stored[1], 16)

            def centre(it, sl):
                dve.wait_ge(loaded[sl], it * 64 + 64)
                for j in range(GC):
                    q = it * (2 * GC) + (sl * GC + j)
                    for k, (t0, t1) in enumerate(((0, 1), (1, NT - 1), (NT - 1, NT))):
                        v = xt[:, sl, j, t0:t1, 1:W + 1]
                        ins = nc.vector.tensor_scalar(
                            v, v, m.row_mean[0:KR, k, ds(q, 1)], None, ALU.subtract)
                    ins.then_inc(centred, 1)

            def stats(it, sl):
                if not statistics:
                    return
                for j in range(GC):
                    q = it * (2 * GC) + (sl * GC + j)
                    dve.wait_ge(evacuated, q + 3)
                    for t in range(NT):
                        ins = nc.vector.bn_stats(m.stat[0:TR, ds(q, 1), t].rearrange("p a k -> p (a k)"),
                                                 yt[:, sl, j, t])
                    ins.then_inc(stat_done, 1)

            centre(0, 0)
            with dve.Fori(0, NG - 1) as it:
                centre(it, 1)
                stats(it, 0)
                centre(it + 1, 0)
                stats(it, 1)
            centre(NG - 1, 1)
            stats(NG - 1, 0)
            stats(NG - 1, 1)


def strips(eng, first, strip, last):
    with eng.Fori(0, B) as s:
        first(s)
        for t in range(CS):
            strip(s, 0, 0, t, 0, True, False)
        with eng.Fori(0, (NCH - 2) // 2) as j:
            for t in range(CS):
                strip(s, j * 2 + 1, j, t, 1, False, False)
            for t in range(CS):
                strip(s, j * 2 + 2, j + 1, t, 0, False, False)
        for t in range(CS):
            strip(s, NCH - 1, (NCH - 1) // 2, t, (NCH - 1) % 2, False, True)
        last(s)


Z0 = 8
STAGES, STAGE0 = 6, 12
ROWS0 = 2
SUMS0 = 3
XSTEPS = 3 + 2 * NCH


def i_of(k, t):
    return k * CS + (t + 1)


def sampled_layer(nc, m, src, dst):
    xs = src.rearrange("b c (k r) w -> (b c) k r w", r=TR)
    ys = dst.rearrange("b c (k r) w -> (b c) k r w", r=TR)
    with ExitStack() as ctx:
        def sem(name):
            return ctx.enter_context(nc.semaphore(name))

        def sb(name, shape):
            return ctx.enter_context(nc.sbuf_tensor(name, shape, F32))

        xc = sb("x_chunks", [128, 2, FR, WP])
        xf = sb("x_first", [128, 4, WP])
        win = sb("windows", [128, 4, NT, WP])
        dif = sb("differences", [128, 2, 4, WP - 1])
        off = sb("offsets", [128, 2, 2, 2, W])
        t1 = sb("term_left", [128, 3, 2, W])
        across = sb("across", [128, 3, 2, W])
        smp = sb("samples", [128, 4, 2, WP])
        out = sb("out_rows", [128, 4, 2, W])
        cols = sb("sample_columns", [128, 3])
        t2 = m.kern[:].rearrange("p q k -> p (q k)").rearrange("p (a b w) -> p a b w", a=3, b=2)
        conv = m.scratch[:, 16:16 + 4 * W].rearrange("p (a b w) -> p a b w", a=2, b=2)
        ready = sem("buffers_ready")
        xf_loaded = sem("x_first_loaded")
        xc_loaded = [sem("x_chunk_loaded0"), sem("x_chunk_loaded1")]
        halo_loaded = sem("last_halo_loaded")
        win_loaded = [sem(f"window_loaded{k}") for k in range(4)]
        win_ready = sem("window_normalized")
        cols_ready = sem("sample_columns_ready")
        z_ready = sem("offset_sums")
        z_free = sem("offsets_copied")
        x_step = sem("x_step")
        mirrored = sem("last_row_mirrored")
        dif_ready = sem("differences_ready")
        stage = sem("sampling_stage")
        edge = sem("edge_sampled")
        smp_ready = sem("samples_ready")
        y_sums = sem("conv_sums")
        y_out = sem("conv_copied")
        rows_ready = sem("rows_ready")
        stats_taken = sem("row_statistics_taken")
        stored = [sem(f"rows_stored{k}") for k in range(4)]
        block = ctx.enter_context(nc.Block())

        @block.sync
        def _(sp):
            sp.wait_ge(ready, 1)

            def load_window(s, i, slot, first=False, last=False):
                for j in range(4):
                    if first and j < 2:
                        sp.dma_start(win[C * j:C * j + C, slot, 1:NT, 1:W + 1],
                                     xs[ds(s * C, C), 0:NT - 1, TR - 2 + j]).then_inc(win_loaded[slot], 16)
                    elif first:
                        sp.dma_start(win[C * j:C * j + C, slot, :, 1:W + 1],
                                     xs[ds(s * C, C), :, j - 2]).then_inc(win_loaded[slot], 16)
                    elif last and j >= 2:
                        sp.dma_start(win[C * j:C * j + C, slot, 0:NT - 1, 1:W + 1],
                                     xs[ds(s * C, C), 1:NT, j - 2]).then_inc(win_loaded[slot], 16)
                    elif last:
                        sp.dma_start(win[C * j:C * j + C, slot, :, 1:W + 1],
                                     xs[ds(s * C, C), :, TR - 2 + j]).then_inc(win_loaded[slot], 16)
                    else:
                        sp.dma_start(win[C * j:C * j + C, slot, :, 1:W + 1],
                                     xs[ds(s * C, C), :, ds(i * 2 + (j - 2), 1)].rearrange("c b r w -> c b (r w)")) \
                            .then_inc(win_loaded[slot], 16)

            def load_chunk(s, k, slot, last=False):
                for b in range(NT):
                    p0 = C * b
                    if last:
                        sp.dma_start(xc[p0:p0 + C, slot, 0:FR - 2, 1:W + 1], xs[ds(s * C, C), b, TR - FR + 2:TR]) \
                            .then_inc(xc_loaded[slot], 16)
                        if b < NT - 1:
                            sp.dma_start(xc[p0:p0 + C, slot, FR - 2:FR, 1:W + 1], xs[ds(s * C, C), b + 1, 0:2]) \
                                .then_inc(halo_loaded, 16)
                    else:
                        sp.dma_start(xc[p0:p0 + C, slot, :, 1:W + 1], xs[ds(s * C, C), b, ds(k * (2 * CS), FR)]) \
                            .then_inc(xc_loaded[slot], 16)

            def store(s, i, slot):
                sp.wait_ge(rows_ready, s * NST + i + ROWS0)
                for b in range(NT):
                    sp.dma_start(ys[ds(s * C, C), b, ds(i * 2 - 2, 2)], out[C * b:C * b + C, slot]) \
                        .then_inc(stored[slot], 16)

            def strip(s, k, t, odd, at_start, at_end):
                i = i_of(k, t)
                sp.wait_ge(z_ready, (s * STRIPS + i) * NT + NT)
                if at_end and t == CS - 1:
                    load_window(s, i, 3, last=True)
                else:
                    load_window(s, i, t % 2)
                if t == 1 and not at_end:
                    sp.wait_ge(rows_ready, s * NST + k * CS + ROWS0)
                    load_chunk(s, k + 1, 1 - odd, last=isinstance(k, int) and k == NCH - 2)
                if not at_start:
                    store(s, i - CS, t)

            with sp.Fori(0, B) as s:
                sp.wait_ge(rows_ready, s * NST + 1)
                for b in range(NT):
                    p0 = C * b
                    sp.dma_start(xf[p0:p0 + C, 2:4, 1:W + 1], xs[ds(s * C, C), b, 0:2]).then_inc(xf_loaded, 16)
                    if b > 0:
                        sp.dma_start(xf[p0:p0 + C, 0:2, 1:W + 1], xs[ds(s * C, C), b - 1, TR - 2:TR]) \
                            .then_inc(xf_loaded, 16)
                sp.wait_ge(z_ready, s * STRIPS * NT + NT)
                load_window(s, 0, 2, first=True)
                load_chunk(s, 0, 0)
                for t in range(CS):
                    strip(s, 0, t, 0, True, False)
                with sp.Fori(0, (NCH - 4) // 2) as j:
                    for t in range(CS):
                        strip(s, j * 2 + 1, t, 1, False, False)
                    for t in range(CS):
                        strip(s, j * 2 + 2, t, 0, False, False)
                for k in range(NCH - 3, NCH):
                    for t in range(CS):
                        strip(s, k, t, k % 2, False, k == NCH - 1)
                for t in range(CS):
                    store(s, NST - CS + 1 + t, t)
            for k in range(4):
                sp.wait_ge(stored[k], 16 * NT * B * NCH + 16)

        @block.scalar
        def _(act):
            act.wait_ge(ready, 1)

            def normalize(s, slot, uses, first=False, last=False):
                act.wait_ge(win_loaded[slot], uses * 64 + 64)
                for j0, j1 in ((0, 2), (2, 4)) if first or last else ((0, 4),):
                    b0 = 1 if first and j0 == 0 else 0
                    b1 = NT - 1 if last and j0 == 2 else NT
                    v = win[C * j0:C * j1, slot, b0:b1, 1:W + 1]
                    ins = nc.scalar.activation(v, v, ACT.Identity, bias=cols[C * j0:C * j1, 0:1],
                                               scale=cols[C * j0:C * j1, 1:2])
                ins.then_inc(win_ready, 1)

            def tanh(s, i, slot, last_use):
                g = s * STRIPS + i
                act.wait_ge(stage, g * STAGES + STAGE0 - STAGES * last_use + STAGES - 1)
                for b in range(NT):
                    act.wait_ge(z_ready, g * NT + b + 1 + Z0)
                    for xy in range(2):
                        for r in range(2):
                            p0 = C * (2 * xy + r)
                            ins = nc.scalar.activation(off[C * b:C * b + C, slot, xy, r, :],
                                                       m.ps[p0:p0 + C, b, 0:W], ACT.Tanh,
                                                       bias=m.half_b_off[p0:p0 + C, 0:1], scale=0.5)
                    ins.then_inc(z_free, 1)

            def copy_out(s, i, par):
                n = s * NST + i
                act.wait_ge(y_sums, n + SUMS0)
                act.wait_ge(rows_ready, n - 2 + ROWS0)
                nc.scalar.activation(conv[:, par], m.ps[:, 4 + 2 * par:6 + 2 * par, 0:W], ACT.Identity,
                                     bias=cols[:, 2:3]).then_inc(y_out, 1)

            def first(s):
                for n, col in enumerate((m.shift_col, m.rstd_col, m.out_bias)):
                    nc.scalar.copy(cols[:, n:n + 1], col[:, ds(s, 1)]).then_inc(cols_ready, 1)
                act.wait_ge(cols_ready, s * 3 + 3)
                normalize(s, 2, s, first=True)
                normalize(s, 0, s * (NST // 2))
                tanh(s, 0, 1, 1)

            def strip(s, k, half, t, odd, at_start, at_end):
                i = i_of(k, t)
                if at_end and t == CS - 2:
                    normalize(s, 3, s, last=True)
                elif not (at_end and t == CS - 1):
                    normalize(s, (t + 1) % 2, s * (NST // 2 - 1 + t % 2) + (k * (CS // 2) + (t + 1) // 2))
                tanh(s, i, t % 2, 2)
                if not (at_start and t == 0):
                    copy_out(s, i - 1, t % 2)

            def last(s):
                copy_out(s, NST, 0)
                act.wait_ge(y_out, s * NST + NST + ROWS0)

            strips(act, first, strip, last)

        @block.tensor
        def _(pe):
            pe.wait_ge(ready, 1)

            def offset_conv(s, i, slot):
                g = s * STRIPS + i
                pe.wait_ge(win_ready, g + 1)
                for b in range(NT):
                    pe.wait_ge(z_free, g * NT + b + 1)
                    for dx in range(3):
                        ins = nc.tensor.matmul(m.ps[:, b, 0:W], m.w_off[:, dx, :],
                                               win[:, slot, b, dx:dx + W], start=(dx == 0), stop=(dx == 2))
                    ins.then_inc(z_ready, 1)

            def last_conv(s, i, t):
                par = (t + 1) % 2
                pe.wait_ge(smp_ready, s * STRIPS + i + 2)
                pe.wait_ge(y_out, s * NST + i - 2 + ROWS0)
                for r in range(2):
                    for tap in range(TAPS):
                        n, dx = r + tap // 3, tap % 3
                        ins = nc.tensor.matmul(m.ps[:, 4 + 2 * par + r, 0:W], m.w_dcn[:, tap, :],
                                               smp[:, (t + n // 2) % 4, n % 2, dx:dx + W],
                                               start=(tap == 0), stop=(tap == TAPS - 1))
                ins.then_inc(y_sums, 1)

            def first(s):
                offset_conv(s, 0, 2)
                offset_conv(s, 1, 0)

            def strip(s, k, half, t, odd, at_start, at_end):
                i = i_of(k, t)
                if not (at_end and t == CS - 1):
                    offset_conv(s, i + 1, 3 if at_end and t == CS - 2 else (t + 1) % 2)
                last_conv(s, i, t)

            strips(pe, first, strip, lambda s: None)

        @block.gpsimd
        def _(pool):
            pool.wait_ge(ready, 1)

            def differences(s, i, slot, last_use, x, step):
                pool.wait_ge(x_step, s * XSTEPS + step)
                pool.wait_ge(stage, (s * STRIPS + i) * STAGES + STAGE0 - STAGES * last_use + 1)
                nc.gpsimd.tensor_tensor(dif[:, slot], x[:, :, 1:WP], x[:, :, 0:WP - 1], ALU.subtract) \
                    .then_inc(dif_ready, 1)

            def first(s):
                differences(s, 0, 1, 1, xf[:], 3)

            def strip(s, k, half, t, odd, at_start, at_end):
                if at_end and t == 0:
                    pool.wait_ge(mirrored, s + 1)
                differences(s, i_of(k, t), t % 2, 2, xc[:, odd, 2 * t:2 * t + 4], k * 2 + 5)

            strips(pool, first, strip, lambda s: None)

        @block.vector
        def _(dve):
            nc.vector.memset(smp[:].rearrange("p a b c -> p (a b c)"), 0.0)
            nc.vector.memset(win[:].rearrange("p a b c -> p (a b c)"), 0.0)
            nc.vector.memset(xc[:].rearrange("p a b c -> p (a b c)"), 0.0)
            for k, (what, n) in enumerate(((z_ready, Z0), (z_free, NT), (stage, STAGE0), (y_sums, SUMS0),
                                           (y_out, ROWS0), (rows_ready, ROWS0), (smp_ready, 1), (stats_taken, 1),
                                           *((one, 16) for one in stored))):
                nc.vector.memset(m.scratch[:, k:k + 1], 0.0).then_inc(what, n)
            nc.vector.memset(xf[:].rearrange("p b c -> p (b c)"), 0.0).then_inc(ready, 1)
            dve.wait_ge(ready, 1)

            def normalize(s, x, step):
                nc.vector.tensor_scalar(x[:, :, 1:W + 1], x[:, :, 1:W + 1], m.mean_col[:, ds(s, 1)],
                                        m.rstd_col[:, ds(s, 1)], ALU.subtract, ALU.mult).then_inc(x_step, 1)
                dve.wait_ge(x_step, s * XSTEPS + step)
                nc.vector.tensor_copy(x[:, :, 0:WP:WP - 1], x[:, :, 2:WP - 2:WP - 5]).then_inc(x_step, 1)

            def sample(s, i, slot, x, sums):
                g = s * STRIPS + i
                st = g * STAGES + STAGE0
                u, v = off[:, slot, 0], off[:, slot, 1]
                dve.wait_ge(smp_ready, g + 1)
                dve.wait_ge(z_free, g * NT + 2 * NT)
                dve.wait_ge(dif_ready, g + 1)
                for r in range(3):
                    nc.vector.scalar_tensor_tensor(out=t1[:, r], in0=u, scalar=0.0, in1=dif[:, slot, r:r + 2, 0:W],
                                                   op0=ALU.max, op1=ALU.mult)
                    ins = nc.vector.scalar_tensor_tensor(out=t2[:, r], in0=u, scalar=0.0,
                                                         in1=dif[:, slot, r:r + 2, 1:W + 1],
                                                         op0=ALU.min, op1=ALU.mult)
                ins.then_inc(stage, 1)
                dve.wait_ge(stage, st + 1)
                nc.vector.tensor_tensor(t1[:], t1[:], t2[:], ALU.add).then_inc(stage, 1)
                dve.wait_ge(stage, st + 2)
                for r in range(3):
                    ins = nc.vector.scalar_tensor_tensor(out=across[:, r], in0=t1[:, r], scalar=-0.5,
                                                         in1=x[:, r:r + 2, 1:W + 1], op0=ALU.mult, op1=ALU.add)
                ins.then_inc(stage, 1)
                dve.wait_ge(stage, st + 3)
                nc.vector.tensor_tensor(t2[:, 0:2], across[:, 1:3], across[:, 0:2], ALU.subtract).then_inc(stage, 1)
                dve.wait_ge(stage, st + 4)
                nc.vector.scalar_tensor_tensor(out=t1[:, 0], in0=v, scalar=0.0, in1=t2[:, 0],
                                               op0=ALU.max, op1=ALU.mult)
                nc.vector.scalar_tensor_tensor(out=t1[:, 1], in0=v, scalar=0.0, in1=t2[:, 1],
                                               op0=ALU.min, op1=ALU.mult).then_inc(stage, 1)
                dve.wait_ge(stage, st + 5)
                nc.vector.tensor_tensor(t1[:, 2], t1[:, 0], t1[:, 1], ALU.add).then_inc(stage, 1)
                dve.wait_ge(stage, st + 6)
                dve.wait_ge(y_sums, s * NST + sums)

            def write_samples(pslot):
                return nc.vector.scalar_tensor_tensor(out=smp[:, pslot, :, 1:W + 1], in0=t1[:, 2], scalar=-0.5,
                                                      in1=across[:, 1], op0=ALU.mult, op1=ALU.add)

            def residual(s, i, par, oslot, uses, x):
                n = s * NST + i
                dve.wait_ge(y_out, n + ROWS0)
                dve.wait_ge(stored[oslot], uses * 64 + 16)
                dve.wait_ge(stats_taken, n)
                nc.vector.scalar_tensor_tensor(out=out[:, oslot], in0=x[:, :, 1:W + 1], scalar=m.std_col[:, ds(s, 1)],
                                               in1=conv[:, par], op0=ALU.mult, op1=ALU.add).then_inc(rows_ready, 1)
                dve.wait_ge(rows_ready, n + ROWS0)
                for r in range(2):
                    ins = nc.vector.bn_stats(m.stat2[:, ds(s, 1), ds(i * 2 + (r - 2), 1)].rearrange("p a b k -> p (a b k)"),
                                       out[:, oslot, r])
                ins.then_inc(stats_taken, 1)

            def first(s):
                dve.wait_ge(xf_loaded, s * 112 + 112)
                normalize(s, xf[:], 1)
                dve.wait_ge(x_step, s * XSTEPS + 2)
                nc.vector.tensor_copy(xf[0:C, 1, :], xf[0:C, 3, :]).then_inc(x_step, 1)
                dve.wait_ge(xc_loaded[0], s * (64 * NCH // 2) + 64)
                normalize(s, xc[:, 0], 4)
                dve.wait_ge(x_step, s * XSTEPS + 5)
                sample(s, 0, 1, xf[:], SUMS0)
                write_samples(0).then_inc(edge, 1)
                dve.wait_ge(edge, s * 2 + 1)
                nc.vector.memset(smp[0:C, 0, 0, 1:W + 1], 0.0).then_inc(smp_ready, 1)

            def strip(s, k, half, t, odd, at_start, at_end):
                i = i_of(k, t)
                if t == 2 and not at_end:
                    dve.wait_ge(xc_loaded[1 - odd], (s * (NCH // 2) + (half + odd)) * 64 + 64)
                    normalize(s, xc[:, 1 - odd], k * 2 + 6)
                if at_end and t == 0:
                    mirror_last_row(s, odd)
                sample(s, i, t % 2, xc[:, odd, 2 * t:2 * t + 4], i)
                if at_end and t == CS - 1:
                    write_samples((t + 1) % 4).then_inc(edge, 1)
                    dve.wait_ge(edge, s * 2 + 2)
                    nc.vector.memset(smp[C * (NT - 1):, (t + 1) % 4, 1, 1:W + 1], 0.0).then_inc(smp_ready, 1)
                else:
                    write_samples((t + 1) % 4).then_inc(smp_ready, 1)
                if t > 0:
                    residual(s, i - 1, t % 2, t - 1, s * NCH + k, xc[:, odd, 2 * t - 2:2 * t])
                elif not at_start:
                    residual(s, i - 1, 0, CS - 1, s * NCH + k - 1, xc[:, 1 - odd, 2 * CS - 2:2 * CS])

            def mirror_last_row(s, odd):
                p0 = C * (NT - 1)
                nc.vector.tensor_copy(xc[p0:, odd, FR - 2, :], xc[p0:, odd, FR - 4, :]).then_inc(mirrored, 1)
                dve.wait_ge(mirrored, s + 1)

            def last(s):
                residual(s, NST, 0, CS - 1, s * NCH + NCH - 1, xc[:, (NCH - 1) % 2, 2 * CS - 2:2 * CS])

            strips(dve, first, strip, last)


def program(nc, x, w1s, b1s, w2s, b2s, w_off, b_off, w_dcn, b_dcn, y):
    with ExitStack() as ctx:
        def sb(name, shape):
            return ctx.enter_context(nc.sbuf_tensor(name, shape, F32))

        m, w = Memory(), Memory()
        m.ps = ctx.enter_context(nc.psum_tensor("ps", [128, 8, 512], F32))
        statistics = sb("statistics", [128, NQ * NT * 6])
        m.stat = statistics[:].rearrange("p (q t k) -> p q t k", t=NT, k=6)
        m.stat2 = statistics[:, 0:B * TR * 6].rearrange("p (s r k) -> p s r k", s=B, k=6)
        m.scratch = sb("scratch", [128, NQ * 2 * NT])
        m.kern = sb("kernels", [128, NQ, TAPS])
        m.ones = sb("ones", [128, 128])
        m.band = sb("band", [128, 3, TR])
        m.sel = sb("channel_select", [128, C])
        m.row_mask = sb("row_mask", [128, 3])
        m.row_mean = sb("row_mean", [128, 3, NQ])
        m.mean, m.rstd, m.chan_mean, m.chan_var, m.row_sum, m.col_sum = (
            sb(name, [128, NQ]) for name in ("mean", "rstd", "chan_mean", "chan_var", "row_sum", "col_sum"))
        m.pair, m.root, m.rough = (sb(name, [128, NQ // 2]) for name in ("pair", "root", "rough"))
        m.mean_col, m.rstd_col, m.std_col, m.shift_col, m.out_bias, m.pooled, m.hidden = (
            sb(name, [128, B]) for name in
            ("mean_col", "rstd_col", "std_col", "shift_col", "out_bias", "pooled", "hidden"))
        m.hidden_wide = sb("hidden_wide", [HID, B, 128])
        m.w_off = sb("w_off", [128, 3, 128])
        m.w_dcn = sb("w_dcn", [128, TAPS, 128])
        m.half_b_off = sb("half_b_off", [128, 1])
        m.b_dcn = sb("b_dcn", [128, 1])
        w.loads = []
        nets = []
        for n in range(3):
            net = Memory()
            net.w1, net.b1 = sb(f"w1_{n}", [C, HID]), sb(f"b1_{n}", [HID, 1])
            net.w2, net.b2 = sb(f"w2_{n}", [HID, C * TAPS]), sb(f"b2_{n}", [128, C * TAPS])
            nets.append(net)
            w.loads += [(net.w1[:], w1s[n]), (net.b1[:], b1s[n].unsqueeze(1)), (net.w2[:], w2s[n]),
                        (net.b2[:], b2s[n].partition_broadcast(128))]
        for r in range(2):
            for dy in range(3):
                for dx in range(3):
                    p0 = C * (r + dy)
                    w.loads.append((m.w_off[p0:p0 + C, dx, :].rearrange("p (a r c) -> p a r c", a=2, r=2)[:, :, r],
                                    w_off[:, dy, dx]))
        for a in range(2):
            for r in range(2):
                p0 = C * (2 * a + r)
                w.loads.append((m.half_b_off[p0:p0 + C], b_off[a].unsqueeze(1)))
        for b in range(4):
            w.loads.append((m.w_dcn[C * b:C * b + C, :, C * b:C * b + C], w_dcn))
            w.loads.append((m.b_dcn[C * b:C * b + C], b_dcn.unsqueeze(1)))
        mid = [nc.dram_tensor(f"layer_{n}", (B, C, H, W), F32, kind="Internal").ap() for n in range(3)]

        setup(nc, m, w)
        input_statistics(nc, m, x)
        parameters(nc, m, 0, False, nets[0])
        depthwise(nc, m, 0, x, mid[0], True)
        parameters(nc, m, 1, False, nets[1])
        depthwise(nc, m, 1, mid[0], mid[1], True)
        parameters(nc, m, 2, False, None)
        sampled_layer(nc, m, mid[1], mid[2])
        parameters(nc, m, 3, True, nets[2])
        depthwise(nc, m, 3, mid[2], y, False)


def kernel(x, L0_conv_w1, L0_conv_b1, L0_conv_w2, L0_conv_b2, L1_conv_w1, L1_conv_b1, L1_conv_w2, L1_conv_b2,
           L2_conv_w_off, L2_conv_b_off, L2_conv_w_dcn, L2_conv_b_dcn,
           L3_conv_w1, L3_conv_b1, L3_conv_w2, L3_conv_b2):
    import numpy as np
    import concourse.bacc as bacc
    from concourse.bass_utils import run_bass_kernel_spmd

    nc = bacc.Bacc("TRN2", target_bir_lowering=False, num_devices=1)
    arrays = {}

    def inp(name, a):
        a = np.ascontiguousarray(a)
        arrays[name] = a
        return nc.dram_tensor(name, a.shape, mybir.dt.from_np(a.dtype), kind="ExternalInput").ap()

    ax = inp("x", x)
    w1s = [inp(f"w1_{n}_in", a) for n, a in enumerate((L0_conv_w1, L1_conv_w1, L3_conv_w1))]
    b1s = [inp(f"b1_{n}_in", a) for n, a in enumerate((L0_conv_b1, L1_conv_b1, L3_conv_b1))]
    w2s = [inp(f"w2_{n}_in", a) for n, a in enumerate((L0_conv_w2, L1_conv_w2, L3_conv_w2))]
    b2s = [inp(f"b2_{n}_in", a) for n, a in enumerate((L0_conv_b2, L1_conv_b2, L3_conv_b2))]
    w_off = inp("w_off_in", np.asarray(L2_conv_w_off).reshape(32, 2, 32, 3, 3).transpose(2, 3, 4, 1, 0))
    b_off = inp("b_off_in", np.asarray(L2_conv_b_off).reshape(32, 2).T)
    w_dcn = inp("w_dcn_in", np.asarray(L2_conv_w_dcn).reshape(32, 32, 9).transpose(1, 2, 0))
    b_dcn = inp("b_dcn_in", L2_conv_b_dcn)
    y = nc.dram_tensor("y", (B, C, H, W), F32, kind="ExternalOutput").ap()
    program(nc, ax, w1s, b1s, w2s, b2s, w_off, b_off, w_dcn, b_dcn, y)
    r = run_bass_kernel_spmd(nc, [arrays], core_ids=[0])
    return r.results[0]["y"]
```

```python
from contextlib import ExitStack

import concourse.bass as bass
from concourse import mybir

F32 = mybir.dt.float32
ALU = mybir.AluOpType
ACT = mybir.ActivationFunctionType
AX_X = mybir.AxisListType.X
ds = bass.ds

B, C, H, W = 8, 32, 384, 384
NQ = B * C
HW = H * W
HID = 128
TAPS = 9
EPS = 1e-5
TR = 96
NT = H // TR
KR = TR + 2
WP = W + 2
GC = 4
HALF = W // 2
PARTS = HW // HALF
NCH = 12
CS = 4
NST = NCH * CS
STRIPS = NST + 1
FR = 2 * CS + 2


class Memory:
    pass


def setup(nc, m, w):
    with nc.semaphore("zeroed") as zeroed, nc.semaphore("weights_loaded") as loaded, \
            nc.semaphore("masks_done") as masks, nc.semaphore("halved") as halved, nc.Block() as block:

        @block.vector
        def _(dve):
            nc.vector.memset(m.w_off[:], 0.0)
            nc.vector.memset(m.w_dcn[:], 0.0)
            nc.vector.memset(m.ones[:], 1.0)
            nc.vector.memset(m.band[:], 0.0)
            nc.vector.memset(m.sel[:], 0.0)
            nc.vector.memset(m.row_mask[:], 1.0).then_inc(zeroed, 1)
            dve.wait_ge(loaded, 16 * len(w.loads))
            nc.vector.tensor_scalar(m.half_b_off[:], m.half_b_off[:], 0.5, None, ALU.mult).then_inc(halved, 1)

        @block.sync
        def _(sp):
            sp.wait_ge(zeroed, 1)
            for dst, src in w.loads:
                sp.dma_start(dst, src).then_inc(loaded, 16)
            sp.wait_ge(loaded, 16 * len(w.loads))

        @block.gpsimd
        def _(pool):
            pool.wait_ge(zeroed, 1)
            for dy in range(3):
                nc.gpsimd.affine_select(out=m.band[:, dy, :], in_=m.band[:, dy, :], compare_op=ALU.not_equal,
                                        fill=1.0, base=-dy, pattern=[[-1, TR]],
                                        channel_multiplier=1).then_inc(masks, 1)
            for b in range(4):
                pool.wait_ge(masks, 3 + b)
                nc.gpsimd.affine_select(out=m.sel[:], in_=m.sel[:], compare_op=ALU.not_equal, fill=1.0,
                                        base=-C * b, pattern=[[-1, C]], channel_multiplier=1).then_inc(masks, 1)
            nc.gpsimd.affine_select(out=m.row_mask[:, 0:1], in_=m.row_mask[:, 0:1], compare_op=ALU.not_equal,
                                    fill=0.0, base=0, pattern=[[0, 1]], channel_multiplier=1).then_inc(masks, 1)
            nc.gpsimd.affine_select(out=m.row_mask[:, 2:3], in_=m.row_mask[:, 2:3], compare_op=ALU.not_equal,
                                    fill=0.0, base=-(KR - 1), pattern=[[0, 1]], channel_multiplier=1).then_inc(masks, 1)
            pool.wait_ge(masks, 9)


def input_statistics(nc, m, x):
    src = x.rearrange("b c (p r) w -> p (b c) (r w)", p=TR)
    with nc.sbuf_tensor("xin", [TR, 2, GC, NT * W], F32) as xin, nc.semaphore("stat_load0") as load0, \
            nc.semaphore("stat_load1") as load1, nc.semaphore("stat_done") as done, nc.Block() as block:
        loaded = [load0, load1]

        @block.sync
        def _(sp):
            with sp.Fori(0, NQ // (2 * GC)) as it:
                for sl in range(2):
                    sp.wait_ge(done, it * 2 + sl + 1)
                    sp.dma_start(xin[:, sl], src[:, ds((it * 2 + sl) * GC, GC)]).then_inc(loaded[sl], 16)

        @block.vector
        def _(dve):
            nc.vector.memset(m.scratch[:, 0:1], 0.0).then_inc(done, 2)
            with dve.Fori(0, NQ // (2 * GC)) as it:
                for sl in range(2):
                    dve.wait_ge(loaded[sl], it * 16 + 16)
                    for j in range(GC):
                        for t in range(NT):
                            ins = nc.vector.bn_stats(
                                m.stat[0:TR, ds((it * 2 + sl) * GC + j, 1), t].rearrange("p a k -> p (a k)"),
                                xin[:, sl, j, t * W:(t + 1) * W])
                    ins.then_inc(done, 1)


def parameters(nc, m, layer, from_blocks, net):
    with ExitStack() as ctx:
        def sem(name):
            return ctx.enter_context(nc.semaphore(f"{name}_{layer}"))

        means_summed, sums = sem("means_summed"), sem("sums")
        vars_summed, var_sums = sem("vars_summed"), sem("var_sums")
        var_ready, sqrt_done = sem("var_ready"), sem("sqrt_done")
        pooled_ready, hidden_sums = sem("pooled_ready"), sem("hidden_sums")
        hidden_ready, kernel_sums = sem("hidden_ready"), sem("kernel_sums")
        step = sem("parameter_step")
        block = ctx.enter_context(nc.Block())
        rows = 4 * C if from_blocks else TR
        if from_blocks:
            part = m.agg[:].unsqueeze(2)
        else:
            part = m.stat[0:TR].rearrange("p q t (e k) -> p q (t e) k", k=3)
        n_col, n_part = part.shape[1], part.shape[2]
        diff = m.scratch[0:rows, 0:n_col * n_part].rearrange("p (q t) -> p q t", t=n_part)

        @block.vector
        def _(dve):
            done = [0]

            def link(ins):
                done[0] += 1
                ins.then_inc(step, 1)
                dve.wait_ge(step, done[0])

            def spread(dst, col):
                nc.vector.tensor_tensor(
                    dst.rearrange("p (s c) -> p s c", c=C), col.unsqueeze(2).broadcast_to([4 * C, B, C]),
                    m.sel[:].unsqueeze(1).broadcast_to([4 * C, B, C]), ALU.mult).then_inc(step, 1)
                done[0] += 1
                dve.wait_ge(step, done[0])

            def column(dst, row):
                tmp = m.scratch[:, 0:NQ].rearrange("p (s c) -> p s c", c=C)
                link(nc.vector.tensor_tensor(tmp, row.rearrange("p (s c) -> p s c", c=C),
                                             m.sel[:].unsqueeze(1).broadcast_to([4 * C, B, C]), ALU.mult))
                link(nc.vector.tensor_reduce(dst, tmp, AX_X, ALU.add))

            if from_blocks:
                spread(m.row_sum[:], m.agg[:, :, 0])
            else:
                link(nc.vector.tensor_reduce(m.col_sum[0:rows, 0:n_col], part[:, :, :, 1], AX_X, ALU.add))
                link(nc.vector.tensor_copy(m.row_sum[0:TR, :], m.col_sum[0:TR, :]))
            nc.vector.memset(m.scratch[:, 0:1], 0.0).then_inc(means_summed, 1)
            dve.wait_ge(sums, 1)
            link(nc.vector.tensor_scalar(m.chan_mean[:], m.ps[:, 0, 0:NQ], 1.0 / (4 if from_blocks else PARTS), None, ALU.mult))
            pair = m.chan_mean[:].rearrange("p (g e) -> p g e", e=2)
            link(nc.vector.tensor_tensor(m.pair[:], pair[:, :, 0], pair[:, :, 1], ALU.add))
            link(nc.vector.tensor_scalar(m.mean[:].rearrange("p (g e) -> p g e", e=2),
                                         m.pair[:].unsqueeze(2).broadcast_to([128, NQ // 2, 2]),
                                         0.5, None, ALU.mult))
            if from_blocks:
                column(m.mean_col[:], m.mean[:])
                middle = m.mean_col[:]
            else:
                middle = m.mean[0:TR, :]
            if from_blocks:
                link(nc.vector.tensor_tensor(m.hidden[:], m.agg[:, :, 0], middle, ALU.subtract))
                link(nc.vector.tensor_tensor(m.hidden[:], m.hidden[:], m.hidden[:], ALU.mult))
                link(nc.vector.tensor_tensor(m.hidden[:], m.hidden[:], m.agg[:, :, 1], ALU.add))
                spread(m.row_sum[:], m.hidden[:])
            else:
                link(nc.vector.tensor_tensor(diff, part[:, :, :, 1],
                                             middle.unsqueeze(2).broadcast_to([rows, n_col, n_part]), ALU.subtract))
                link(nc.vector.tensor_tensor(diff, diff, diff, ALU.mult))
                link(nc.vector.scalar_tensor_tensor(out=diff, in0=diff, scalar=float(HALF), in1=part[:, :, :, 2],
                                                    op0=ALU.mult, op1=ALU.add))
                link(nc.vector.tensor_reduce(m.col_sum[0:rows, 0:n_col], diff, AX_X, ALU.add))
                link(nc.vector.tensor_copy(m.row_sum[0:TR, :], m.col_sum[0:TR, :]))
            nc.vector.memset(m.scratch[:, 0:1], 0.0).then_inc(vars_summed, 1)
            dve.wait_ge(var_sums, 1)
            link(nc.vector.tensor_copy(m.chan_var[:], m.ps[:, 1, 0:NQ]))
            pair = m.chan_var[:].rearrange("p (g e) -> p g e", e=2)
            link(nc.vector.tensor_tensor(m.pair[:], pair[:, :, 0], pair[:, :, 1], ALU.add))
            link(nc.vector.tensor_scalar(m.pair[:], m.pair[:], 1.0 / (8 if from_blocks else 2 * HW), EPS, ALU.mult, ALU.add))
            nc.vector.memset(m.scratch[:, 0:1], 0.0).then_inc(var_ready, 1)
            dve.wait_ge(sqrt_done, 1)
            link(nc.vector.reciprocal(m.rough[:], m.root[:]))
            link(nc.vector.tensor_tensor(m.root[:], m.rough[:], m.rough[:], ALU.mult))
            link(nc.vector.tensor_tensor(m.root[:], m.root[:], m.pair[:], ALU.mult))
            link(nc.vector.tensor_scalar(m.root[:], m.root[:], -0.5, 1.5, ALU.mult, ALU.add))
            link(nc.vector.tensor_tensor(m.rough[:], m.rough[:], m.root[:], ALU.mult))
            link(nc.vector.tensor_copy(m.rstd[:].rearrange("p (g e) -> p g e", e=2),
                                       m.rough[:].unsqueeze(2).broadcast_to([128, NQ // 2, 2])))
            if net is None:
                column(m.mean_col[:], m.mean[:])
                column(m.rstd_col[:], m.rstd[:])
                link(nc.vector.tensor_tensor(m.shift_col[:], m.mean_col[:], m.rstd_col[:], ALU.mult))
                link(nc.vector.tensor_scalar(m.shift_col[:], m.shift_col[:], -1.0, None, ALU.mult))
                return
            for k in range(3):
                link(nc.vector.tensor_scalar(m.row_mean[:, k], m.mean[:], m.row_mask[:, k:k + 1], None, ALU.mult))
            link(nc.vector.tensor_tensor(m.chan_mean[:], m.chan_mean[:], m.mean[:], ALU.subtract))
            link(nc.vector.tensor_tensor(m.chan_mean[:], m.chan_mean[:], m.rstd[:], ALU.mult))
            column(m.pooled[:], m.chan_mean[:])
            nc.vector.memset(m.scratch[:, 0:1], 0.0).then_inc(pooled_ready, 1)
            dve.wait_ge(hidden_sums, 1)
            link(nc.vector.tensor_scalar(m.hidden[:], m.ps[:, 2, 0:B], net.b1[:, 0:1], 0.0, ALU.add, ALU.max))
            nc.vector.tensor_copy(m.hidden_wide[:], m.hidden[:].unsqueeze(2).broadcast_to([HID, B, 128])) \
                .then_inc(hidden_ready, 1)
            dve.wait_ge(kernel_sums, 1)
            kern = m.kern[:].rearrange("p (s c) k -> p s (c k)", s=B)
            link(nc.vector.tensor_tensor(kern, m.ps[:, :, 0:C * TAPS],
                                         net.b2[:].unsqueeze(1).broadcast_to([128, B, C * TAPS]), ALU.add))
            link(nc.vector.tensor_tensor(m.kern[:], m.kern[:],
                                         m.rstd[:].unsqueeze(2).broadcast_to([128, NQ, TAPS]), ALU.mult))
            link(nc.vector.tensor_scalar(m.kern[:, :, TAPS // 2], m.kern[:, :, TAPS // 2], 1.0, None, ALU.add))

        @block.tensor
        def _(pe):
            pe.wait_ge(means_summed, 1)
            nc.tensor.matmul(m.ps[:, 0, 0:NQ], m.ones[0:rows, :], m.row_sum[0:rows, :], start=True, stop=True) \
                .then_inc(sums, 1)
            pe.wait_ge(vars_summed, 1)
            nc.tensor.matmul(m.ps[:, 1, 0:NQ], m.ones[0:rows, :], m.row_sum[0:rows, :], start=True, stop=True) \
                .then_inc(var_sums, 1)
            if net is None:
                return
            pe.wait_ge(pooled_ready, 1)
            nc.tensor.matmul(m.ps[:, 2, 0:B], net.w1[:, :], m.pooled[0:C, :], start=True, stop=True) \
                .then_inc(hidden_sums, 1)
            pe.wait_ge(hidden_ready, 1)
            for s in range(B):
                ins = nc.tensor.matmul(m.ps[:, s, 0:C * TAPS], m.hidden_wide[:, s, :], net.w2[:, :],
                                       start=True, stop=True)
            ins.then_inc(kernel_sums, 1)

        @block.scalar
        def _(act):
            act.wait_ge(var_ready, 1)
            nc.scalar.activation(m.root[:], m.pair[:], ACT.Sqrt).then_inc(sqrt_done, 1)


def depthwise(nc, m, layer, src, dst, statistics):
    xs = src.rearrange("b c h w -> h (b c) w")
    ys = dst.rearrange("b c (t p) w -> p (b c) t w", p=TR)
    with ExitStack() as ctx:
        def sem(name):
            return ctx.enter_context(nc.semaphore(f"{name}_{layer}"))

        def sb(name, shape):
            return ctx.enter_context(nc.sbuf_tensor(f"{name}_{layer}", shape, F32))

        xt = sb("x_tiles", [KR, 2, GC, NT, WP])
        yt = sb("y_tiles", [TR, 2, GC, NT, W])
        mat = sb("banded", [KR, 4, 3, TR])
        term = sb("banded_terms", [KR, 2, 3, TR])
        pads_zero = sem("pads_zero")
        loaded = [sem("x_loaded0"), sem("x_loaded1")]
        stored = [sem("y_stored0"), sem("y_stored1")]
        centred = sem("centred")
        built = sem("matrices_built")
        build_step = sem("build_step")
        conv_done = sem("conv_done")
        evacuated = sem("evacuated")
        stat_done = sem("stat_done")
        block = ctx.enter_context(nc.Block())
        NG = NQ // (2 * GC)

        @block.sync
        def _(sp):
            sp.wait_ge(pads_zero, 3)
            with sp.Fori(0, NG) as it:
                for sl in range(2):
                    q0 = (it * 2 + sl) * GC
                    sp.wait_ge(conv_done, q0 + 4)
                    for t in range(NT):
                        lo, hi = max(t * TR - 1, 0), min(t * TR + TR + 1, H)
                        p0 = lo - (t * TR - 1)
                        sp.dma_start(xt[p0:p0 + hi - lo, sl, :, t, 1:W + 1], xs[lo:hi, ds(q0, GC)]) \
                            .then_inc(loaded[sl], 16)

        @block.gpsimd
        def _(pool):
            with pool.Fori(0, NG) as it:
                for j in range(2 * GC):
                    q = it * (2 * GC) + j

                    def tap(dy):
                        return m.kern[0:KR, ds(q, 1), 3 * dy:3 * dy + 3].rearrange("p a k -> p (a k)") \
                            .unsqueeze(2).broadcast_to([KR, 3, TR])

                    def band(dy):
                        return m.band[0:KR, dy, :].unsqueeze(1).broadcast_to([KR, 3, TR])

                    pool.wait_ge(conv_done, q + 5)
                    nc.gpsimd.tensor_tensor(mat[:, j % 4], band(0), tap(0), ALU.mult)
                    nc.gpsimd.tensor_tensor(term[:, 0], band(1), tap(1), ALU.mult)
                    nc.gpsimd.tensor_tensor(term[:, 1], band(2), tap(2), ALU.mult).then_inc(build_step, 1)
                    pool.wait_ge(build_step, q * 2 + 1)
                    nc.gpsimd.tensor_tensor(mat[:, j % 4], mat[:, j % 4], term[:, 0], ALU.add) \
                        .then_inc(build_step, 1)
                    pool.wait_ge(build_step, q * 2 + 2)
                    nc.gpsimd.tensor_tensor(mat[:, j % 4], mat[:, j % 4], term[:, 1], ALU.add).then_inc(built, 1)
                    pool.wait_ge(built, q + 1)

        @block.tensor
        def _(pe):
            with pe.Fori(0, NG) as it:
                for j in range(2 * GC):
                    q = it * (2 * GC) + j
                    pe.wait_ge(centred, q + 1)
                    pe.wait_ge(built, q + 1)
                    pe.wait_ge(evacuated, q + 1)
                    for dx in range(3):
                        for t in range(NT):
                            ins = nc.tensor.matmul(m.ps[0:TR, 4 * (j % 2) + t, 0:W], mat[:, j % 4, dx, :],
                                                   xt[:, j // GC, j % GC, t, dx:dx + W],
                                                   start=(dx == 0), stop=(dx == 2))
                    ins.then_inc(conv_done, 1)

        @block.scalar
        def _(act):
            with act.Fori(0, NG) as it:
                for j in range(2 * GC):
                    q = it * (2 * GC) + j
                    sl = j // GC
                    if j % GC == 0:
                        act.wait_ge(stored[sl], it * 64 + 16)
                        if statistics:
                            act.wait_ge(stat_done, q + 4)
                    act.wait_ge(conv_done, q + 9)
                    act.wait_ge(pads_zero, 3)
                    nc.scalar.activation(yt[:, sl, j % GC], m.ps[0:TR, 4 * (j % 2):4 * (j % 2) + 4, 0:W],
                                         ACT.Identity, bias=m.mean[0:TR, ds(q, 1)]).then_inc(evacuated, 1)
                    act.wait_ge(evacuated, q + 3)
                    act.dma_start(ys[:, ds(q, 1)].rearrange("p a t w -> p (a t) w"), yt[:, sl, j % GC]) \
                        .then_inc(stored[sl], 16)
            for sl in range(2):
                act.wait_ge(stored[sl], NG * 64 + 16)

        @block.vector
        def _(dve):
            nc.vector.memset(xt[:, :, :, :, 0:WP:WP - 1].rearrange("p a b c d -> p (a b c) d"), 0.0) \
                .then_inc(pads_zero, 1)
            dve.wait_ge(pads_zero, 1)
            nc.vector.memset(xt[0:1, :, :, 0, :].rearrange("p a b d -> p (a b) d"), 0.0).then_inc(pads_zero, 1)
            dve.wait_ge(pads_zero, 2)
            nc.vector.memset(xt[TR:KR, :, :, NT - 1, :].rearrange("p a b d -> p (a b) d"), 0.0) \
                .then_inc(pads_zero, 1)
            nc.vector.memset(m.scratch[:, 0:1], 0.0).then_inc(conv_done, 8)
            nc.vector.memset(m.scratch[:, 1:2], 0.0).then_inc(evacuated, 2)
            nc.vector.memset(m.scratch[:, 2:3], 0.0).then_inc(stat_done, 8)
            nc.vector.memset(m.scratch[:, 3:4], 0.0).then_inc(stored[0], 16)
            nc.vector.memset(m.scratch[:, 4:5], 0.0).then_inc(stored[1], 16)

            def centre(it, sl):
                dve.wait_ge(loaded[sl], it * 64 + 64)
                for j in range(GC):
                    q = it * (2 * GC) + (sl * GC + j)
                    for k, (t0, t1) in enumerate(((0, 1), (1, NT - 1), (NT - 1, NT))):
                        v = xt[:, sl, j, t0:t1, 1:W + 1]
                        ins = nc.vector.tensor_scalar(
                            v, v, m.row_mean[0:KR, k, ds(q, 1)], None, ALU.subtract)
                    ins.then_inc(centred, 1)

            def stats(it, sl):
                if not statistics:
                    return
                for j in range(GC):
                    q = it * (2 * GC) + (sl * GC + j)
                    dve.wait_ge(evacuated, q + 3)
                    for t in range(NT):
                        ins = nc.vector.bn_stats(m.stat[0:TR, ds(q, 1), t].rearrange("p a k -> p (a k)"),
                                                 yt[:, sl, j, t])
                    ins.then_inc(stat_done, 1)

            centre(0, 0)
            with dve.Fori(0, NG - 1) as it:
                centre(it, 1)
                stats(it, 0)
                centre(it + 1, 0)
                stats(it, 1)
            centre(NG - 1, 1)
            stats(NG - 1, 0)
            stats(NG - 1, 1)


class Strip:

    def __init__(self, s, j, c):
        self.s, self.j, self.c = s, j, c
        self.i = j * 8 + c
        self.half = j * 4 + c // 2
        self.use = j * 4 + (c - 1) // 2
        self.g = s * STRIPS + self.i
        self.n = s * NST + self.i
        self.k = j * 2 + (c - 1) // CS
        self.odd = (c - 1) // CS % 2
        self.t = (c - 1) % CS


def before(strip, lag, carry):
    c = strip.c - lag
    if c >= 0:
        return None if strip.s is END else Strip(strip.s, strip.j, c)
    if not carry:
        return None
    return Strip(B - 1 if strip.s is END else strip.s - 1, 0, STRIPS + c)


END = "end"


class Tail:

    def __init__(self, c):
        self.s, self.c = END, c


def stream(eng, step, lags):
    def copy(value, first, last):
        if isinstance(value, int):
            return value
        reg = eng.alloc_register()
        eng.reg_mov(reg, value)
        return eng.snap(reg, min_val=first, max_val=last)

    def strip(s, j, c, carry):
        step(Strip(copy(s, 1, B - 1), copy(j, 0, (NST - 16) // 8 - 1), c), carry)

    def sample(s, carry):
        for c in range(9):
            strip(s, 0, c, carry)
        with eng.Fori(0, (NST - 16) // 8) as j:
            for c in range(9, 17):
                strip(s, j, c, carry)
        for c in range(NST - 7, NST + 1):
            strip(s, 0, c, carry)

    sample(0, False)
    with eng.Fori(1, B) as s:
        sample(s, True)
    for c in range(lags):
        step(Tail(c), True)


XSTEPS = 3 + 2 * NCH
Z0 = 2 * NT
T0 = 2
V0 = 4
A0 = 4
S0 = 2
Y0 = 2


def sampled_layer(nc, m, src, dst):
    xs = src.rearrange("b c (k r) w -> (b c) k r w", r=TR)
    ys = dst.rearrange("b c (k r) w -> (b c) k r w", r=TR)
    z = nc.dram_tensor("sampled_rows", (B * STRIPS, 2, C, NT, W), F32, kind="Internal").ap()
    with ExitStack() as ctx:
        def sem(name):
            return ctx.enter_context(nc.semaphore(name))

        def sb(name, shape):
            return ctx.enter_context(nc.sbuf_tensor(name, shape, F32))

        xc = sb("x_chunks", [128, 2, FR, WP])
        xf = sb("x_first", [128, 4, WP])
        win = sb("windows", [128, 4, NT, WP])
        dif = sb("differences", [128, 2, 4, WP - 1])
        offx = sb("offsets_x", [128, 2, 2, W])
        offy = sb("offsets_y", [128, 5, 2, W])
        t1 = sb("term_left", [128, 3, 2, W])
        t3 = sb("terms", [128, 3, 2, W])
        smp = sb("samples", [128, 2, 2, W])
        win2 = sb("sample_windows", [128, 2, NT, WP])
        out = sb("out_rows", [128, 2, 2, W])
        cols = sb("sample_columns", [128, 2])
        moments = sb("moments", [128, 2])
        rows6 = sb("row_statistics", [128, TR, 6])

        t2 = m.kern[:].rearrange("p q k -> p (q k)").rearrange("p (a b w) -> p a b w", a=3, w=W)
        flat = m.stat_flat
        across = flat[:, 0:12 * W].rearrange("p (a b w) -> p a b w", a=6, w=W)
        down = flat[:, 12 * W:16 * W].rearrange("p (a b w) -> p a b w", a=2, w=W)
        weighed_rows = m.scratch[:, 16:16 + 4 * W].rearrange("p (a b w) -> p a b w", a=2, w=W)
        xr = [m.row_mean[:].rearrange("p a q -> p (a q)")[:, 0:2 * W].rearrange("p (a w) -> p a w", w=W),
              m.hidden_wide[:].rearrange("p a q -> p (a q)")[:, 0:2 * W].rearrange("p (a w) -> p a w", w=W)]

        ready = sem("buffers_ready")
        xf_loaded = sem("x_first_loaded")
        xc_loaded = [sem("x_chunk_loaded0"), sem("x_chunk_loaded1")]
        halo_loaded = sem("last_halo_loaded")
        win_loaded = [sem(f"window_loaded{k}") for k in range(4)]
        win_ready = sem("window_normalized")
        cols_ready = sem("sample_columns_ready")
        z_ready = sem("offset_sums")
        z_free = sem("offsets_copied")
        x_step = sem("x_step")
        mirrored = sem("last_row_mirrored")
        dif_ready = sem("differences_ready")
        terms_ready = sem("terms_ready")
        terms_added = sem("terms_added")
        across_ready = sem("across_ready")
        down_ready = sem("down_ready")
        weighed = sem("down_weighed")
        weighed_sum = sem("down_weighed_sum")
        edge = sem("edge_sampled")
        smp_ready = sem("samples_ready")
        smp_stored = [sem("samples_stored0"), sem("samples_stored1")]
        win2_loaded = [sem("sample_window0"), sem("sample_window1")]
        y_sums = sem("conv_sums")
        xr_loaded = [sem("residual_loaded0"), sem("residual_loaded1")]
        rows_ready = sem("rows_ready")
        stats_taken = sem("row_statistics_taken")
        moments_ready = sem("moments_ready")
        aggregated = sem("statistics_aggregated")
        stored = [sem("rows_stored0"), sem("rows_stored1")]
        block = ctx.enter_context(nc.Block())

        def window_slot(a):
            return {0: 2, NST: 3}.get(a.c, (a.c - 1) % 2)

        @block.sync
        def _(sp):
            sp.wait_ge(ready, 1)

            def store_samples(a):
                sp.wait_ge(smp_ready, a.g + 1 + S0)
                for b in range(NT):
                    sp.dma_start(z[ds(a.g, 1), :, :, b].rearrange("a r c w -> c (a r) w"),
                                 smp[C * b:C * b + C, a.c % 2]).then_inc(smp_stored[a.c % 2], 16)

            def store_rows(a):
                sp.wait_ge(rows_ready, a.n + Y0)
                for bl in range(2):
                    for r in range(2):
                        p0 = C * (2 * bl + r)
                        sp.dma_start(ys[ds(a.s * C, C), bl:NT:2, ds(a.i * 2 + (r - 2), 1)]
                                     .rearrange("c b r w -> c b (r w)"), out[p0:p0 + C, a.c % 2]) \
                            .then_inc(stored[a.c % 2], 16)

            def load_sample_window(a):
                sp.wait_ge(y_sums, a.n - 2 + Y0)
                if a.c == 1:
                    sp.wait_ge(smp_stored[0], a.s * (64 * (NST // 2 + 1)) + 64 + 16)
                n = NST // 2 + 1 - a.c % 2
                sp.wait_ge(smp_stored[a.c % 2], (a.s * n + a.half) * 64 + 64 + 16)
                sp.dma_start(win2[:, a.c % 2, :, 1:W + 1],
                             z[ds(a.g - 1, 2)].rearrange("a r c b w -> (a r c) b w")) \
                    .then_inc(win2_loaded[a.c % 2], 16)

            def load_residual(a):
                sp.wait_ge(rows_ready, a.n - 2 + Y0)
                for bl in range(2):
                    for r in range(2):
                        p0 = C * (2 * bl + r)
                        sp.dma_start(xr[a.c % 2][p0:p0 + C], xs[ds(a.s * C, C), bl:NT:2, ds(a.i * 2 + (r - 2), 1)]
                                     .rearrange("c b r w -> c b (r w)")).then_inc(xr_loaded[a.c % 2], 16)

            def load_window(a):
                sp.wait_ge(z_ready, (a.g - 1) * NT + Z0)
                slot = window_slot(a)
                for j in range(4):
                    b0, b1, d0, r = 0, NT, 0, j - 2
                    if a.c == 0 and j < 2:
                        b1, d0, r = NT - 1, 1, TR - 2 + j
                    if a.c == NST:
                        b0, r = (0, TR - 2 + j) if j < 2 else (1, j - 2)
                    rows = xs[ds(a.s * C, C), b0:b1, r] if a.c in (0, NST) else \
                        xs[ds(a.s * C, C), :, ds(a.i * 2 + r, 1)].rearrange("c b r w -> c b (r w)")
                    sp.dma_start(win[C * j:C * j + C, slot, d0:d0 + b1 - b0, 1:W + 1], rows) \
                        .then_inc(win_loaded[slot], 16)

            def load_chunk(a):
                sp.wait_ge(across_ready, a.g + (1 - CS - 1 + A0))
                for b in range(NT):
                    p0 = C * b
                    if a.c == NST - CS + 1:
                        sp.dma_start(xc[p0:p0 + C, a.odd, 0:FR - 2, 1:W + 1], xs[ds(a.s * C, C), b, TR - FR + 2:TR]) \
                            .then_inc(xc_loaded[a.odd], 16)
                        if b < NT - 1:
                            sp.dma_start(xc[p0:p0 + C, a.odd, FR - 2:FR, 1:W + 1], xs[ds(a.s * C, C), b + 1, 0:2]) \
                                .then_inc(halo_loaded, 16)
                    else:
                        sp.dma_start(xc[p0:p0 + C, a.odd, :, 1:W + 1],
                                     xs[ds(a.s * C, C), b, ds(a.k * (2 * CS), FR)]).then_inc(xc_loaded[a.odd], 16)

            def load_first(s):
                sp.wait_ge(across_ready, s * STRIPS + 1)
                for b in range(NT):
                    p0 = C * b
                    sp.dma_start(xf[p0:p0 + C, 2:4, 1:W + 1], xs[ds(s * C, C), b, 0:2]).then_inc(xf_loaded, 16)
                    if b > 0:
                        sp.dma_start(xf[p0:p0 + C, 0:2, 1:W + 1], xs[ds(s * C, C), b - 1, TR - 2:TR]) \
                            .then_inc(xf_loaded, 16)
                for b in range(NT):
                    sp.dma_start(xc[C * b:C * b + C, 0, :, 1:W + 1], xs[ds(s * C, C), b, 0:FR]) \
                        .then_inc(xc_loaded[0], 16)

            def step(a, carry):
                smp6, row8, res5 = before(a, 6, carry), before(a, 8, carry), before(a, 5, carry)
                if smp6:
                    store_samples(smp6)
                if row8 and row8.c:
                    store_rows(row8)
                if smp6 and smp6.c:
                    load_sample_window(smp6)
                if res5 and res5.c:
                    load_residual(res5)
                if a.s is END:
                    return
                load_window(a)
                if a.c == 0:
                    load_first(a.s)
                elif a.c > 1 and a.t == 0:
                    load_chunk(a)

            stream(sp, step, 8)
            for k in range(2):
                sp.wait_ge(stored[k], 64 * B * NST // 2 + 16)

        @block.scalar
        def _(act):
            act.wait_ge(ready, 1)

            def normalize(a):
                slot = window_slot(a)
                uses = {0: a.s * (NST // 2), 1: a.s * (NST // 2 - 1)}
                act.wait_ge(win_loaded[slot], (uses[slot] + a.use if slot < 2 else a.s) * 64 + 64)
                for j0, j1 in ((0, 2), (2, 4)) if slot > 1 else ((0, 4),):
                    b0 = 1 if a.c == 0 and j0 == 0 else 0
                    b1 = NT - 1 if a.c == NST and j0 == 2 else NT
                    v = win[C * j0:C * j1, slot, b0:b1, 1:W + 1]
                    ins = nc.scalar.activation(v, v, ACT.Identity, bias=cols[C * j0:C * j1, 0:1],
                                               scale=cols[C * j0:C * j1, 1:2])
                ins.then_inc(win_ready, 1)

            def tanh(a):
                act.wait_ge(terms_ready, a.g - 2 + 1 + T0 + (a.c == 0))
                act.wait_ge(weighed, a.g - 4 + 1 + V0)
                dst = (offx[:, a.c % 2], offy[:, a.c % 4 if a.c else 4])
                for b in range(NT):
                    act.wait_ge(z_ready, a.g * NT + b + 1 + Z0)
                    for xy in range(2):
                        for r in range(2):
                            p0 = C * (2 * xy + r)
                            ins = nc.scalar.activation(dst[xy][C * b:C * b + C, r, :],
                                                       m.ps[p0:p0 + C, b, 0:W], ACT.Tanh,
                                                       bias=m.half_b_off[p0:p0 + C, 0:1], scale=0.5)
                    ins.then_inc(z_free, 1)

            def step(a, carry):
                if a.c == 0 and a.s is not END:
                    if carry:
                        act.wait_ge(win_ready, a.g + 1)
                        tanh(before(a, 1, carry))
                    for n, col in enumerate((m.shift_col, m.rstd_col)):
                        nc.scalar.copy(cols[:, n:n + 1], col[:, ds(a.s, 1)]).then_inc(cols_ready, 1)
                    act.wait_ge(cols_ready, a.s * 2 + 2)
                    normalize(a)
                    return
                if a.s is not END:
                    normalize(a)
                tanh(before(a, 1, carry))

            stream(act, step, 1)

        @block.tensor
        def _(pe):
            pe.wait_ge(ready, 1)

            def offset_conv(a):
                pe.wait_ge(win_ready, a.g + 2)
                for b in range(NT):
                    pe.wait_ge(z_free, a.g * NT + b + 1)
                    for dx in range(3):
                        ins = nc.tensor.matmul(m.ps[:, b, 0:W], m.w_off[:, dx, :],
                                               win[:, window_slot(a), b, dx:dx + W], start=(dx == 0), stop=(dx == 2))
                    ins.then_inc(z_ready, 1)

            def last_conv(a):
                pe.wait_ge(win2_loaded[a.c % 2], (a.s * (NST // 2) + a.use) * 16 + 16)
                pe.wait_ge(rows_ready, a.n - 2 + Y0)
                for bh in range(2):
                    for dx in range(3):
                        for bl in range(2):
                            ins = nc.tensor.matmul(m.ps[64 * bl:64 * bl + 64, 4 + 2 * (a.c % 2) + bh, 0:W],
                                                   m.w_dcn[:, dx, :],
                                                   win2[:, a.c % 2, 2 * bh + bl, dx:dx + W],
                                                   start=(dx == 0), stop=(dx == 2))
                ins.then_inc(y_sums, 1)

            def step(a, carry):
                if a.s is not END:
                    offset_conv(a)
                conv4 = before(a, 4, carry)
                if conv4 and conv4.c:
                    last_conv(conv4)

            stream(pe, step, 4)

        def rows_of(a):
            return xc[:, a.odd, 2 * a.t:2 * a.t + 4] if a.c else xf[:]

        @block.gpsimd
        def _(pool):
            pool.wait_ge(ready, 1)

            def differences(a):
                pool.wait_ge(x_step, a.s * XSTEPS + (a.k * 2 + 5 if a.c else 3))
                if a.c == NST - CS + 1:
                    pool.wait_ge(mirrored, a.s + 1)
                pool.wait_ge(terms_ready, a.g - 2 + 1 + T0 + (a.c == 0))
                x = rows_of(a)
                nc.gpsimd.tensor_tensor(dif[:, a.c % 2], x[:, :, 1:WP], x[:, :, 0:WP - 1], ALU.subtract) \
                    .then_inc(dif_ready, 1)

            def add_terms(a):
                pool.wait_ge(terms_ready, a.g + 1 + T0)
                pool.wait_ge(across_ready, a.g + A0)
                nc.gpsimd.tensor_tensor(t3[:], t1[:], t2[:], ALU.add).then_inc(terms_added, 1)

            def differences_down(a):
                pool.wait_ge(across_ready, a.g + 1 + A0)
                pool.wait_ge(weighed, a.g + V0)
                r = 3 * (a.c % 2)
                nc.gpsimd.tensor_tensor(down, across[:, r + 1:r + 3], across[:, r:r + 2], ALU.subtract) \
                    .then_inc(down_ready, 1)

            def step(a, carry):
                if a.s is not END:
                    differences(a)
                add1, down2 = before(a, 1, carry), before(a, 2, carry)
                if add1:
                    add_terms(add1)
                if down2:
                    differences_down(down2)

            stream(pool, step, 2)

        @block.vector
        def _(dve):
            nc.vector.memset(win2[:].rearrange("p a b c -> p (a b c)"), 0.0)
            nc.vector.memset(win[:].rearrange("p a b c -> p (a b c)"), 0.0)
            nc.vector.memset(xc[:].rearrange("p a b c -> p (a b c)"), 0.0)
            for k, (what, n) in enumerate(((win_ready, 1), (z_ready, Z0), (z_free, NT), (terms_ready, T0),
                                           (terms_added, 1), (across_ready, A0), (weighed, V0), (smp_ready, S0),
                                           (y_sums, Y0), (rows_ready, Y0), (stats_taken, Y0), (aggregated, 1),
                                           *((one, 16) for one in smp_stored + stored))):
                nc.vector.memset(m.scratch[:, k:k + 1], 0.0).then_inc(what, n)
            nc.vector.memset(xf[:].rearrange("p b c -> p (b c)"), 0.0).then_inc(ready, 1)
            dve.wait_ge(ready, 1)

            def normalize(s, x, step):
                nc.vector.tensor_scalar(x[:, :, 1:W + 1], x[:, :, 1:W + 1], m.mean_col[:, ds(s, 1)],
                                        m.rstd_col[:, ds(s, 1)], ALU.subtract, ALU.mult).then_inc(x_step, 1)
                dve.wait_ge(x_step, s * XSTEPS + step)
                nc.vector.tensor_copy(x[:, :, 0:WP:WP - 1], x[:, :, 2:WP - 2:WP - 5]).then_inc(x_step, 1)
                dve.wait_ge(x_step, s * XSTEPS + step + 1)

            def normalize_first(s):
                dve.wait_ge(xf_loaded, s * 112 + 112)
                normalize(s, xf[:], 1)
                nc.vector.tensor_copy(xf[0:C, 1, :], xf[0:C, 3, :]).then_inc(x_step, 1)
                dve.wait_ge(x_step, s * XSTEPS + 3)
                dve.wait_ge(xc_loaded[0], s * (64 * NCH // 2) + 64)
                normalize(s, xc[:, 0], 4)

            def normalize_next(a):
                odd = 1 - a.odd
                half = a.j + ((a.c - 1) // CS + 1) // 2
                dve.wait_ge(xc_loaded[odd], (a.s * (NCH // 2) + half) * 64 + 64)
                if a.c == NST - CS - 1:
                    dve.wait_ge(halo_loaded, a.s * 48 + 48)
                normalize(a.s, xc[:, odd], a.k * 2 + 6)
                if a.c == NST - CS - 1:
                    p0 = C * (NT - 1)
                    nc.vector.tensor_copy(xc[p0:, odd, FR - 2, :], xc[p0:, odd, FR - 4, :]).then_inc(mirrored, 1)
                    dve.wait_ge(mirrored, a.s + 1)

            def terms(a):
                dve.wait_ge(z_free, a.g * NT + 2 * NT)
                dve.wait_ge(dif_ready, a.g + 1)
                dve.wait_ge(terms_added, a.g + 1)
                u, d = offx[:, a.c % 2], dif[:, a.c % 2]
                for r in range(3):
                    nc.vector.scalar_tensor_tensor(out=t1[:, r], in0=u, scalar=0.0, in1=d[:, r:r + 2, 0:W],
                                                   op0=ALU.max, op1=ALU.mult)
                    ins = nc.vector.scalar_tensor_tensor(out=t2[:, r], in0=u, scalar=0.0, in1=d[:, r:r + 2, 1:W + 1],
                                                         op0=ALU.min, op1=ALU.mult)
                ins.then_inc(terms_ready, 1)

            def sample_across(a):
                dve.wait_ge(terms_added, a.g + 2)
                dve.wait_ge(smp_ready, a.g - 2 + 1 + S0 + (a.c == 0))
                x = rows_of(a)
                for r in range(3):
                    ins = nc.vector.scalar_tensor_tensor(out=across[:, 3 * (a.c % 2) + r], in0=t3[:, r], scalar=-0.5,
                                                         in1=x[:, r:r + 2, 1:W + 1], op0=ALU.mult, op1=ALU.add)
                ins.then_inc(across_ready, 1)

            def weigh_down(a):
                dve.wait_ge(down_ready, a.g + 1)
                dve.wait_ge(smp_ready, a.g + S0)
                v = offy[:, a.c % 4 if a.c else 4]
                nc.vector.scalar_tensor_tensor(out=weighed_rows[:, 0], in0=v, scalar=0.0, in1=down[:, 0],
                                               op0=ALU.max, op1=ALU.mult)
                nc.vector.scalar_tensor_tensor(out=weighed_rows[:, 1], in0=v, scalar=0.0, in1=down[:, 1],
                                               op0=ALU.min, op1=ALU.mult).then_inc(weighed, 1)

            def add_down(a):
                dve.wait_ge(weighed, a.g + 1 + V0)
                nc.vector.tensor_tensor(weighed_rows[:, 0], weighed_rows[:, 0], weighed_rows[:, 1], ALU.add) \
                    .then_inc(weighed_sum, 1)

            def sample(a):
                dve.wait_ge(weighed_sum, a.g + 1)
                n = NST // 2 + 1 - a.c % 2
                dve.wait_ge(smp_stored[a.c % 2], (a.s * n + a.half) * 64 + 16)
                ins = nc.vector.scalar_tensor_tensor(out=smp[:, a.c % 2], in0=weighed_rows[:, 0], scalar=-0.5,
                                                     in1=across[:, 3 * (a.c % 2) + 1], op0=ALU.mult, op1=ALU.add)
                if a.c in (0, NST):
                    r, p0 = (0, 0) if a.c == 0 else (1, C * (NT - 1))
                    ins.then_inc(edge, 1)
                    dve.wait_ge(edge, a.s * 2 + (1 if a.c == 0 else 2))
                    ins = nc.vector.memset(smp[p0:p0 + C, 0, r], 0.0)
                ins.then_inc(smp_ready, 1)

            def residual(a):
                dve.wait_ge(y_sums, a.n + Y0)
                dve.wait_ge(xr_loaded[a.c % 2], (a.s * (NST // 2) + a.use) * 64 + 64)
                dve.wait_ge(stored[a.c % 2], (a.s * (NST // 2) + a.use) * 64 + 16)
                dve.wait_ge(stats_taken, a.n - 2 + Y0)
                y = m.ps[:, 4 + 2 * (a.c % 2):6 + 2 * (a.c % 2), 0:W]
                nc.vector.scalar_tensor_tensor(out=out[:, a.c % 2], in0=y, scalar=m.b_dcn[:, 0:1], in1=xr[a.c % 2],
                                               op0=ALU.add, op1=ALU.add).then_inc(rows_ready, 1)

            def statistics(a):
                dve.wait_ge(rows_ready, a.n + Y0)
                if a.c == 1:
                    dve.wait_ge(aggregated, a.s + 1)
                for h in range(2):
                    ins = nc.vector.bn_stats(
                        rows6[:, ds(a.i * 2 + (h - 2), 1)].rearrange("p a k -> p (a k)"), out[:, a.c % 2, h])
                ins.then_inc(stats_taken, 1)
                if a.c == NST:
                    dve.wait_ge(stats_taken, a.n + Y0)
                    nc.vector.memset(m.scratch[:, 15:16], 0.0)
                    nc.vector.bn_aggr(moments[:], rows6[:].rearrange("p r k -> p (r k)")).then_inc(moments_ready, 1)
                    dve.wait_ge(moments_ready, a.s + 1)
                    nc.vector.tensor_copy(m.agg[:, ds(a.s, 1)].rearrange("p a k -> p (a k)"), moments[:]) \
                        .then_inc(aggregated, 1)

            def step(a, carry):
                row4, down2, across1 = before(a, 4, carry), before(a, 2, carry), before(a, 1, carry)
                if a.s is not END:
                    if a.c == 0:
                        normalize_first(a.s)
                    terms(a)
                if row4 and row4.c:
                    residual(row4)
                if down2:
                    weigh_down(down2)
                late = across1 and across1.c == 0
                if across1 and not late:
                    sample_across(across1)
                if down2:
                    add_down(down2)
                if row4 and row4.c:
                    statistics(row4)
                if down2:
                    sample(down2)
                if late:
                    sample_across(across1)
                if a.s is not END and a.c % CS == CS - 1 and a.c < NST - CS:
                    normalize_next(a)

            stream(dve, step, 4)


def program(nc, x, w1s, b1s, w2s, b2s, w_off, b_off, w_dcn, b_dcn, y):
    with ExitStack() as ctx:
        def sb(name, shape):
            return ctx.enter_context(nc.sbuf_tensor(name, shape, F32))

        m, w = Memory(), Memory()
        m.ps = ctx.enter_context(nc.psum_tensor("ps", [128, 8, 512], F32))
        statistics = sb("statistics", [128, NQ * NT * 6])
        m.stat = statistics[:].rearrange("p (q t k) -> p q t k", t=NT, k=6)
        m.stat_flat = statistics[:]
        m.agg = sb("sample_statistics", [128, B, 2])
        m.scratch = sb("scratch", [128, NQ * 2 * NT])
        m.kern = sb("kernels", [128, NQ, TAPS])
        m.ones = sb("ones", [128, 128])
        m.band = sb("band", [128, 3, TR])
        m.sel = sb("channel_select", [128, C])
        m.row_mask = sb("row_mask", [128, 3])
        m.row_mean = sb("row_mean", [128, 3, NQ])
        m.mean, m.rstd, m.chan_mean, m.chan_var, m.row_sum, m.col_sum = (
            sb(name, [128, NQ]) for name in ("mean", "rstd", "chan_mean", "chan_var", "row_sum", "col_sum"))
        m.pair, m.root, m.rough = (sb(name, [128, NQ // 2]) for name in ("pair", "root", "rough"))
        m.mean_col, m.rstd_col, m.shift_col, m.pooled, m.hidden = (
            sb(name, [128, B]) for name in
            ("mean_col", "rstd_col", "shift_col", "pooled", "hidden"))
        m.hidden_wide = sb("hidden_wide", [HID, B, 128])
        m.w_off = sb("w_off", [128, 3, 128])
        m.w_dcn = sb("w_dcn", [128, 3, 2 * C])
        m.half_b_off = sb("half_b_off", [128, 1])
        m.b_dcn = sb("b_dcn", [128, 1])
        w.loads = []
        nets = []
        for n in range(3):
            net = Memory()
            net.w1, net.b1 = sb(f"w1_{n}", [C, HID]), sb(f"b1_{n}", [HID, 1])
            net.w2, net.b2 = sb(f"w2_{n}", [HID, C * TAPS]), sb(f"b2_{n}", [128, C * TAPS])
            nets.append(net)
            w.loads += [(net.w1[:], w1s[n]), (net.b1[:], b1s[n].unsqueeze(1)), (net.w2[:], w2s[n]),
                        (net.b2[:], b2s[n].partition_broadcast(128))]
        for r in range(2):
            for dy in range(3):
                for dx in range(3):
                    p0 = C * (r + dy)
                    w.loads.append((m.w_off[p0:p0 + C, dx, :].rearrange("p (a r c) -> p a r c", a=2, r=2)[:, :, r],
                                    w_off[:, dy, dx]))
        for r in range(2):
            for dy in range(3):
                p0 = C * (r + dy)
                w.loads.append((m.w_dcn[p0:p0 + C, :, C * r:C * r + C], w_dcn[:, dy]))
        for a in range(2):
            for r in range(2):
                p0 = C * (2 * a + r)
                w.loads.append((m.half_b_off[p0:p0 + C], b_off[a].unsqueeze(1)))
        for b in range(4):
            w.loads.append((m.b_dcn[C * b:C * b + C], b_dcn.unsqueeze(1)))
        mid = [nc.dram_tensor(f"layer_{n}", (B, C, H, W), F32, kind="Internal").ap() for n in range(3)]

        setup(nc, m, w)
        input_statistics(nc, m, x)
        parameters(nc, m, 0, False, nets[0])
        depthwise(nc, m, 0, x, mid[0], True)
        parameters(nc, m, 1, False, nets[1])
        depthwise(nc, m, 1, mid[0], mid[1], True)
        parameters(nc, m, 2, False, None)
        sampled_layer(nc, m, mid[1], mid[2])
        parameters(nc, m, 3, True, nets[2])
        depthwise(nc, m, 3, mid[2], y, False)


def kernel(x, L0_conv_w1, L0_conv_b1, L0_conv_w2, L0_conv_b2, L1_conv_w1, L1_conv_b1, L1_conv_w2, L1_conv_b2,
           L2_conv_w_off, L2_conv_b_off, L2_conv_w_dcn, L2_conv_b_dcn,
           L3_conv_w1, L3_conv_b1, L3_conv_w2, L3_conv_b2):
    import numpy as np
    import concourse.bacc as bacc
    from concourse.bass_utils import run_bass_kernel_spmd

    nc = bacc.Bacc("TRN2", target_bir_lowering=False, num_devices=1)
    arrays = {}

    def inp(name, a):
        a = np.ascontiguousarray(a)
        arrays[name] = a
        return nc.dram_tensor(name, a.shape, mybir.dt.from_np(a.dtype), kind="ExternalInput").ap()

    ax = inp("x", x)
    w1s = [inp(f"w1_{n}_in", a) for n, a in enumerate((L0_conv_w1, L1_conv_w1, L3_conv_w1))]
    b1s = [inp(f"b1_{n}_in", a) for n, a in enumerate((L0_conv_b1, L1_conv_b1, L3_conv_b1))]
    w2s = [inp(f"w2_{n}_in", a) for n, a in enumerate((L0_conv_w2, L1_conv_w2, L3_conv_w2))]
    b2s = [inp(f"b2_{n}_in", a) for n, a in enumerate((L0_conv_b2, L1_conv_b2, L3_conv_b2))]
    w_off = inp("w_off_in", np.asarray(L2_conv_w_off).reshape(32, 2, 32, 3, 3).transpose(2, 3, 4, 1, 0))
    b_off = inp("b_off_in", np.asarray(L2_conv_b_off).reshape(32, 2).T)
    w_dcn = inp("w_dcn_in", np.asarray(L2_conv_w_dcn).transpose(1, 2, 3, 0))
    b_dcn = inp("b_dcn_in", L2_conv_b_dcn)
    y = nc.dram_tensor("y", (B, C, H, W), F32, kind="ExternalOutput").ap()
    program(nc, ax, w1s, b1s, w2s, b2s, w_off, b_off, w_dcn, b_dcn, y)
    r = run_bass_kernel_spmd(nc, [arrays], core_ids=[0])
    return r.results[0]["y"]
```

```python
from contextlib import ExitStack

import concourse.bass as bass
from concourse import mybir

F32 = mybir.dt.float32
F32R = mybir.dt.float32r
ALU = mybir.AluOpType
ACT = mybir.ActivationFunctionType
AX_X = mybir.AxisListType.X
ds = bass.ds

B, C, H, W = 8, 32, 384, 384
NQ = B * C
HW = H * W
HID = 128
TAPS = 9
EPS = 1e-5
TR = 96
NT = H // TR
KR = TR + 2
WP = W + 2
GC = 4
RING = 4
HALF = W // 2
PARTS = HW // HALF
NCH = 12
CS = 4
NST = NCH * CS
STRIPS = NST + 1
FR = 2 * CS + 2


class Memory:
    pass


def setup(nc, m, w):
    with nc.semaphore("zeroed") as zeroed, nc.semaphore("weights_loaded") as loaded, \
            nc.semaphore("masks_done") as masks, nc.semaphore("halved") as halved, nc.Block() as block:

        @block.vector
        def _(dve):
            nc.vector.memset(m.w_off[:], 0.0)
            nc.vector.memset(m.w_dcn[:], 0.0)
            nc.vector.memset(m.ones[:], 1.0)
            nc.vector.memset(m.band[:], 0.0)
            nc.vector.memset(m.sel[:], 0.0)
            nc.vector.memset(m.row_mask[:], 1.0).then_inc(zeroed, 1)
            dve.wait_ge(loaded, 16 * len(w.loads))
            nc.vector.tensor_scalar(m.half_b_off[:], m.half_b_off[:], 0.5, None, ALU.mult).then_inc(halved, 1)

        @block.sync
        def _(sp):
            sp.wait_ge(zeroed, 1)
            for dst, src in w.loads:
                sp.dma_start(dst, src).then_inc(loaded, 16)
            sp.wait_ge(loaded, 16 * len(w.loads))

        @block.gpsimd
        def _(pool):
            pool.wait_ge(zeroed, 1)
            for dy in range(3):
                nc.gpsimd.affine_select(out=m.band[:, dy, :], in_=m.band[:, dy, :], compare_op=ALU.not_equal,
                                        fill=1.0, base=-dy, pattern=[[-1, TR]],
                                        channel_multiplier=1).then_inc(masks, 1)
            for b in range(4):
                pool.wait_ge(masks, 3 + b)
                nc.gpsimd.affine_select(out=m.sel[:], in_=m.sel[:], compare_op=ALU.not_equal, fill=1.0,
                                        base=-C * b, pattern=[[-1, C]], channel_multiplier=1).then_inc(masks, 1)
            nc.gpsimd.affine_select(out=m.row_mask[:, 0:1], in_=m.row_mask[:, 0:1], compare_op=ALU.not_equal,
                                    fill=0.0, base=0, pattern=[[0, 1]], channel_multiplier=1).then_inc(masks, 1)
            nc.gpsimd.affine_select(out=m.row_mask[:, 2:3], in_=m.row_mask[:, 2:3], compare_op=ALU.not_equal,
                                    fill=0.0, base=-(KR - 1), pattern=[[0, 1]], channel_multiplier=1).then_inc(masks, 1)
            pool.wait_ge(masks, 9)


def input_statistics(nc, m, x):
    src = x.rearrange("b c (p r) w -> p (b c) (r w)", p=TR)
    with nc.sbuf_tensor("xin", [TR, 2, GC, NT * W], F32) as xin, nc.semaphore("stat_load0") as load0, \
            nc.semaphore("stat_load1") as load1, nc.semaphore("stat_done") as done, nc.Block() as block:
        loaded = [load0, load1]

        @block.sync
        def _(sp):
            with sp.Fori(0, NQ // (2 * GC)) as it:
                for sl in range(2):
                    sp.wait_ge(done, it * 2 + sl + 1)
                    sp.dma_start(xin[:, sl], src[:, ds((it * 2 + sl) * GC, GC)]).then_inc(loaded[sl], 16)

        @block.vector
        def _(dve):
            nc.vector.memset(m.scratch[:, 0:1], 0.0).then_inc(done, 2)
            with dve.Fori(0, NQ // (2 * GC)) as it:
                for sl in range(2):
                    dve.wait_ge(loaded[sl], it * 16 + 16)
                    for j in range(GC):
                        for t in range(NT):
                            ins = nc.vector.bn_stats(
                                m.stat[0:TR, ds((it * 2 + sl) * GC + j, 1), t].rearrange("p a k -> p (a k)"),
                                xin[:, sl, j, t * W:(t + 1) * W])
                    ins.then_inc(done, 1)


def parameters(nc, m, layer, from_blocks, net):
    with ExitStack() as ctx:
        def sem(name):
            return ctx.enter_context(nc.semaphore(f"{name}_{layer}"))

        means_summed, sums = sem("means_summed"), sem("sums")
        vars_summed, var_sums = sem("vars_summed"), sem("var_sums")
        var_ready, sqrt_done = sem("var_ready"), sem("sqrt_done")
        pooled_ready, hidden_sums = sem("pooled_ready"), sem("hidden_sums")
        hidden_ready, kernel_sums = sem("hidden_ready"), sem("kernel_sums")
        step = sem("parameter_step")
        block = ctx.enter_context(nc.Block())
        rows = 4 * C if from_blocks else TR
        if from_blocks:
            part = m.agg[:].unsqueeze(2)
        else:
            part = m.stat[0:TR].rearrange("p q t (e k) -> p q (t e) k", k=3)
        n_col, n_part = part.shape[1], part.shape[2]
        diff = m.scratch[0:rows, 0:n_col * n_part].rearrange("p (q t) -> p q t", t=n_part)

        @block.vector
        def _(dve):
            done = [0]

            def link(ins):
                done[0] += 1
                ins.then_inc(step, 1)
                dve.wait_ge(step, done[0])

            def spread(dst, col):
                nc.vector.tensor_tensor(
                    dst.rearrange("p (s c) -> p s c", c=C), col.unsqueeze(2).broadcast_to([4 * C, B, C]),
                    m.sel[:].unsqueeze(1).broadcast_to([4 * C, B, C]), ALU.mult).then_inc(step, 1)
                done[0] += 1
                dve.wait_ge(step, done[0])

            def column(dst, row):
                tmp = m.scratch[:, 0:NQ].rearrange("p (s c) -> p s c", c=C)
                link(nc.vector.tensor_tensor(tmp, row.rearrange("p (s c) -> p s c", c=C),
                                             m.sel[:].unsqueeze(1).broadcast_to([4 * C, B, C]), ALU.mult))
                link(nc.vector.tensor_reduce(dst, tmp, AX_X, ALU.add))

            if from_blocks:
                spread(m.row_sum[:], m.agg[:, :, 0])
            else:
                link(nc.vector.tensor_reduce(m.col_sum[0:rows, 0:n_col], part[:, :, :, 1], AX_X, ALU.add))
                link(nc.vector.tensor_copy(m.row_sum[0:TR, :], m.col_sum[0:TR, :]))
            nc.vector.memset(m.scratch[:, 0:1], 0.0).then_inc(means_summed, 1)
            dve.wait_ge(sums, 1)
            link(nc.vector.tensor_scalar(m.chan_mean[:], m.ps[:, 0, 0:NQ], 1.0 / (4 if from_blocks else PARTS), None, ALU.mult))
            pair = m.chan_mean[:].rearrange("p (g e) -> p g e", e=2)
            link(nc.vector.tensor_tensor(m.pair[:], pair[:, :, 0], pair[:, :, 1], ALU.add))
            link(nc.vector.tensor_scalar(m.mean[:].rearrange("p (g e) -> p g e", e=2),
                                         m.pair[:].unsqueeze(2).broadcast_to([128, NQ // 2, 2]),
                                         0.5, None, ALU.mult))
            if from_blocks:
                column(m.mean_col[:], m.mean[:])
                middle = m.mean_col[:]
            else:
                middle = m.mean[0:TR, :]
            if from_blocks:
                link(nc.vector.tensor_tensor(m.hidden[:], m.agg[:, :, 0], middle, ALU.subtract))
                link(nc.vector.tensor_tensor(m.hidden[:], m.hidden[:], m.hidden[:], ALU.mult))
                link(nc.vector.tensor_tensor(m.hidden[:], m.hidden[:], m.agg[:, :, 1], ALU.add))
                spread(m.row_sum[:], m.hidden[:])
            else:
                link(nc.vector.tensor_tensor(diff, part[:, :, :, 1],
                                             middle.unsqueeze(2).broadcast_to([rows, n_col, n_part]), ALU.subtract))
                link(nc.vector.tensor_tensor(diff, diff, diff, ALU.mult))
                link(nc.vector.scalar_tensor_tensor(out=diff, in0=diff, scalar=float(HALF), in1=part[:, :, :, 2],
                                                    op0=ALU.mult, op1=ALU.add))
                link(nc.vector.tensor_reduce(m.col_sum[0:rows, 0:n_col], diff, AX_X, ALU.add))
                link(nc.vector.tensor_copy(m.row_sum[0:TR, :], m.col_sum[0:TR, :]))
            nc.vector.memset(m.scratch[:, 0:1], 0.0).then_inc(vars_summed, 1)
            dve.wait_ge(var_sums, 1)
            link(nc.vector.tensor_copy(m.chan_var[:], m.ps[:, 1, 0:NQ]))
            pair = m.chan_var[:].rearrange("p (g e) -> p g e", e=2)
            link(nc.vector.tensor_tensor(m.pair[:], pair[:, :, 0], pair[:, :, 1], ALU.add))
            link(nc.vector.tensor_scalar(m.pair[:], m.pair[:], 1.0 / (8 if from_blocks else 2 * HW), EPS, ALU.mult, ALU.add))
            nc.vector.memset(m.scratch[:, 0:1], 0.0).then_inc(var_ready, 1)
            dve.wait_ge(sqrt_done, 1)
            link(nc.vector.reciprocal(m.rough[:], m.root[:]))
            link(nc.vector.tensor_tensor(m.root[:], m.rough[:], m.rough[:], ALU.mult))
            link(nc.vector.tensor_tensor(m.root[:], m.root[:], m.pair[:], ALU.mult))
            link(nc.vector.tensor_scalar(m.root[:], m.root[:], -0.5, 1.5, ALU.mult, ALU.add))
            link(nc.vector.tensor_tensor(m.rough[:], m.rough[:], m.root[:], ALU.mult))
            link(nc.vector.tensor_copy(m.rstd[:].rearrange("p (g e) -> p g e", e=2),
                                       m.rough[:].unsqueeze(2).broadcast_to([128, NQ // 2, 2])))
            if net is None:
                column(m.mean_col[:], m.mean[:])
                column(m.rstd_col[:], m.rstd[:])
                link(nc.vector.tensor_tensor(m.shift_col[:], m.mean_col[:], m.rstd_col[:], ALU.mult))
                link(nc.vector.tensor_scalar(m.shift_col[:], m.shift_col[:], -1.0, None, ALU.mult))
                return
            for k in range(3):
                link(nc.vector.tensor_scalar(m.row_mean[:, k], m.mean[:], m.row_mask[:, k:k + 1], None, ALU.mult))
            link(nc.vector.tensor_tensor(m.chan_mean[:], m.chan_mean[:], m.mean[:], ALU.subtract))
            link(nc.vector.tensor_tensor(m.chan_mean[:], m.chan_mean[:], m.rstd[:], ALU.mult))
            column(m.pooled[:], m.chan_mean[:])
            nc.vector.memset(m.scratch[:, 0:1], 0.0).then_inc(pooled_ready, 1)
            dve.wait_ge(hidden_sums, 1)
            link(nc.vector.tensor_scalar(m.hidden[:], m.ps[:, 2, 0:B], net.b1[:, 0:1], 0.0, ALU.add, ALU.max))
            nc.vector.tensor_copy(m.hidden_wide[:], m.hidden[:].unsqueeze(2).broadcast_to([HID, B, 128])) \
                .then_inc(hidden_ready, 1)
            dve.wait_ge(kernel_sums, 1)
            kern = m.kern[:].rearrange("p (s c) k -> p s (c k)", s=B)
            link(nc.vector.tensor_tensor(kern, m.ps[:, :, 0:C * TAPS],
                                         net.b2[:].unsqueeze(1).broadcast_to([128, B, C * TAPS]), ALU.add))
            link(nc.vector.tensor_tensor(m.kern[:], m.kern[:],
                                         m.rstd[:].unsqueeze(2).broadcast_to([128, NQ, TAPS]), ALU.mult))
            link(nc.vector.tensor_scalar(m.kern[:, :, TAPS // 2], m.kern[:, :, TAPS // 2], 1.0, None, ALU.add))

        @block.tensor
        def _(pe):
            pe.wait_ge(means_summed, 1)
            nc.tensor.matmul(m.ps[:, 0, 0:NQ], m.ones[0:rows, :], m.row_sum[0:rows, :], start=True, stop=True) \
                .then_inc(sums, 1)
            pe.wait_ge(vars_summed, 1)
            nc.tensor.matmul(m.ps[:, 1, 0:NQ], m.ones[0:rows, :], m.row_sum[0:rows, :], start=True, stop=True) \
                .then_inc(var_sums, 1)
            if net is None:
                return
            pe.wait_ge(pooled_ready, 1)
            nc.tensor.matmul(m.ps[:, 2, 0:B], net.w1[:, :], m.pooled[0:C, :], start=True, stop=True) \
                .then_inc(hidden_sums, 1)
            pe.wait_ge(hidden_ready, 1)
            for s in range(B):
                ins = nc.tensor.matmul(m.ps[:, s, 0:C * TAPS], m.hidden_wide[:, s, :], net.w2[:, :],
                                       start=True, stop=True)
            ins.then_inc(kernel_sums, 1)

        @block.scalar
        def _(act):
            act.wait_ge(var_ready, 1)
            nc.scalar.activation(m.root[:], m.pair[:], ACT.Sqrt).then_inc(sqrt_done, 1)


def depthwise(nc, m, layer, src, dst, statistics):
    xs = src.rearrange("b c h w -> h (b c) w")
    ys = dst.rearrange("b c (t p) w -> p (b c) t w", p=TR)
    with ExitStack() as ctx:
        def sem(name):
            return ctx.enter_context(nc.semaphore(f"{name}_{layer}"))

        def sb(name, shape):
            return ctx.enter_context(nc.sbuf_tensor(f"{name}_{layer}", shape, F32))

        def sb_parts(name, shape):
            return ctx.enter_context(nc.sbuf_tensor(f"{name}_{layer}", shape, F32R))

        xt = sb("x_tiles", [KR, 2, GC, NT, WP])
        x_hi, x_lo = sb_parts("x_high", [KR, RING, NT, WP]), sb_parts("x_low", [KR, RING, NT, WP])
        yt = sb("y_tiles", [TR, RING, NT, W])
        banded = sb("banded", [KR, 3, TR])
        term = sb("banded_terms", [KR, 2, 3, TR])
        mat_hi, mat_lo = (sb_parts(name, [KR, RING, 3, TR]) for name in ("banded_high", "banded_low"))
        pads_zero = sem("pads_zero")
        loaded = [sem("x_loaded0"), sem("x_loaded1")]
        stored = [sem(f"y_stored{k}") for k in range(RING)]
        centred = sem("centred")
        high_ready = sem("high_parts_ready")
        split = sem("split")
        built = sem("matrices_built")
        build_step = sem("build_step")
        conv_done = sem("conv_done")
        evacuated = sem("evacuated")
        stat_done = sem("stat_done")
        block = ctx.enter_context(nc.Block())
        NG = NQ // (2 * GC)

        def channel_steps(eng, step):
            for j in range(2 * GC):
                step(0, j)
            with eng.Fori(1, NG - 1) as it:
                for j in range(2 * GC):
                    step(it, j)
            for j in range(2 * GC):
                step(NG - 1, j)

        def moved(it, j, by):
            it, j = it + (j + by) // (2 * GC), (j + by) % (2 * GC)
            return (it, j) if not isinstance(it, int) or 0 <= it < NG else None

        @block.sync
        def _(sp):
            sp.wait_ge(pads_zero, 3)
            with sp.Fori(0, NG) as it:
                for sl in range(2):
                    q0 = (it * 2 + sl) * GC
                    sp.wait_ge(split, q0 + 4)
                    for t in range(NT):
                        lo, hi = max(t * TR - 1, 0), min(t * TR + TR + 1, H)
                        p0 = lo - (t * TR - 1)
                        sp.dma_start(xt[p0:p0 + hi - lo, sl, :, t, 1:W + 1], xs[lo:hi, ds(q0, GC)]) \
                            .then_inc(loaded[sl], 16)

        @block.gpsimd
        def _(pool):
            with pool.Fori(0, NG) as it:
                for j in range(2 * GC):
                    q = it * (2 * GC) + j

                    def tap(dy):
                        return m.kern[0:KR, ds(q, 1), 3 * dy:3 * dy + 3].rearrange("p a k -> p (a k)") \
                            .unsqueeze(2).broadcast_to([KR, 3, TR])

                    def band(dy):
                        return m.band[0:KR, dy, :].unsqueeze(1).broadcast_to([KR, 3, TR])

                    nc.gpsimd.tensor_tensor(banded[:], band(0), tap(0), ALU.mult)
                    nc.gpsimd.tensor_tensor(term[:, 0], band(1), tap(1), ALU.mult)
                    nc.gpsimd.tensor_tensor(term[:, 1], band(2), tap(2), ALU.mult).then_inc(build_step, 1)
                    pool.wait_ge(build_step, q * 4 + 1)
                    nc.gpsimd.tensor_tensor(banded[:], banded[:], term[:, 0], ALU.add).then_inc(build_step, 1)
                    pool.wait_ge(build_step, q * 4 + 2)
                    pool.wait_ge(conv_done, q + 1)
                    nc.gpsimd.tensor_tensor(mat_hi[:, j % RING], banded[:], term[:, 1], ALU.add) \
                        .then_inc(build_step, 1)
                    pool.wait_ge(build_step, q * 4 + 3)
                    nc.gpsimd.tensor_tensor(banded[:], banded[:], term[:, 1], ALU.add).then_inc(build_step, 1)
                    pool.wait_ge(build_step, q * 4 + 4)
                    nc.gpsimd.tensor_tensor(mat_lo[:, j % RING], banded[:], mat_hi[:, j % RING], ALU.subtract) \
                        .then_inc(built, 1)
                    pool.wait_ge(built, q + 1)

        @block.tensor
        def _(pe):
            with pe.Fori(0, NG) as it:
                for j in range(2 * GC):
                    q = it * (2 * GC) + j
                    r = j % RING
                    pe.wait_ge(split, q + 1 + 8)
                    pe.wait_ge(built, q + 1)
                    pe.wait_ge(evacuated, q + 1)
                    for dx in range(3):
                        for n, (a, x) in enumerate(((mat_hi, x_hi), (mat_hi, x_lo), (mat_lo, x_hi))):
                            for t in range(NT):
                                ins = nc.tensor.matmul(m.ps[0:TR, 4 * (j % 2) + t, 0:W], a[:, r, dx, :],
                                                       x[:, r, t, dx:dx + W],
                                                       start=(dx == 0 and n == 0), stop=(dx == 2 and n == 2))
                    ins.then_inc(conv_done, 1)

        @block.scalar
        def _(act):
            def high_part(it, j):
                q = it * (2 * GC) + j
                act.wait_ge(centred, q + 1)
                act.wait_ge(conv_done, q + 1)
                nc.scalar.copy(x_hi[:, j % RING], xt[:, j // GC, j % GC]).then_inc(high_ready, 1)

            def step(it, j):
                q = it * (2 * GC) + j
                r = j % RING
                ahead = moved(it, j, 2)
                if ahead:
                    high_part(*ahead)
                act.wait_ge(stored[r], (it * 2 + j // GC) * 16 + 16)
                if statistics:
                    act.wait_ge(stat_done, q + 1)
                act.wait_ge(conv_done, q + 1 + RING)
                act.wait_ge(pads_zero, 3)
                nc.scalar.activation(yt[:, r], m.ps[0:TR, 4 * (j % 2):4 * (j % 2) + 4, 0:W],
                                     ACT.Identity, bias=m.mean[0:TR, ds(q, 1)]).then_inc(evacuated, 1)
                act.wait_ge(evacuated, q + 3)
                act.dma_start(ys[:, ds(q, 1)].rearrange("p a t w -> p (a t) w"), yt[:, r]).then_inc(stored[r], 16)

            high_part(0, 0)
            high_part(0, 1)
            channel_steps(act, step)
            for r in range(RING):
                act.wait_ge(stored[r], NQ // RING * 16 + 16)

        @block.vector
        def _(dve):
            nc.vector.memset(xt[:, :, :, :, 0:WP:WP - 1].rearrange("p a b c d -> p (a b c) d"), 0.0) \
                .then_inc(pads_zero, 1)
            dve.wait_ge(pads_zero, 1)
            nc.vector.memset(xt[0:1, :, :, 0, :].rearrange("p a b d -> p (a b) d"), 0.0).then_inc(pads_zero, 1)
            dve.wait_ge(pads_zero, 2)
            nc.vector.memset(xt[TR:KR, :, :, NT - 1, :].rearrange("p a b d -> p (a b) d"), 0.0) \
                .then_inc(pads_zero, 1)
            for k, (what, n) in enumerate(((conv_done, RING), (evacuated, 2), (stat_done, RING), (split, 8),
                                           *((one, 16) for one in stored))):
                nc.vector.memset(m.scratch[:, k:k + 1], 0.0).then_inc(what, n)

            def centre(it, j):
                q = it * (2 * GC) + j
                if j % GC == 0:
                    dve.wait_ge(loaded[j // GC], it * 64 + 64)
                for k, (t0, t1) in enumerate(((0, 1), (1, NT - 1), (NT - 1, NT))):
                    v = xt[:, j // GC, j % GC, t0:t1, 1:W + 1]
                    ins = nc.vector.tensor_scalar(v, v, m.row_mean[0:KR, k, ds(q, 1)], None, ALU.subtract)
                ins.then_inc(centred, 1)

            def low_part(it, j):
                dve.wait_ge(high_ready, it * (2 * GC) + (j + 1))
                nc.vector.tensor_tensor(x_lo[:, j % RING], xt[:, j // GC, j % GC], x_hi[:, j % RING],
                                        ALU.subtract).then_inc(split, 1)

            def stats(it, j):
                q = it * (2 * GC) + j
                dve.wait_ge(evacuated, q + 3)
                for t in range(NT):
                    ins = nc.vector.bn_stats(m.stat[0:TR, ds(q, 1), t].rearrange("p a k -> p (a k)"),
                                             yt[:, j % RING, t])
                ins.then_inc(stat_done, 1)

            def step(it, j):
                for work, by in ((centre, 3), (low_part, 2), (stats, -1)):
                    other = moved(it, j, by)
                    if other and (statistics or work is not stats):
                        work(*other)

            for j in range(3):
                centre(0, j)
            low_part(0, 0)
            low_part(0, 1)
            channel_steps(dve, step)
            if statistics:
                stats(NG - 1, 2 * GC - 1)


class Strip:

    def __init__(self, s, j, c):
        self.s, self.j, self.c = s, j, c
        self.i = j * 8 + c
        self.half = j * 4 + c // 2
        self.use = j * 4 + (c - 1) // 2
        self.g = s * STRIPS + self.i
        self.n = s * NST + self.i
        self.k = j * 2 + (c - 1) // CS
        self.odd = (c - 1) // CS % 2
        self.t = (c - 1) % CS


def before(strip, lag, carry):
    c = strip.c - lag
    if c >= 0:
        return None if strip.s is END else Strip(strip.s, strip.j, c)
    if not carry:
        return None
    return Strip(B - 1 if strip.s is END else strip.s - 1, 0, STRIPS + c)


END = "end"


class Tail:

    def __init__(self, c):
        self.s, self.c = END, c


def stream(eng, step, lags):
    def copy(value, first, last):
        if isinstance(value, int):
            return value
        reg = eng.alloc_register()
        eng.reg_mov(reg, value)
        return eng.snap(reg, min_val=first, max_val=last)

    def strip(s, j, c, carry):
        step(Strip(copy(s, 1, B - 1), copy(j, 0, (NST - 16) // 8 - 1), c), carry)

    def sample(s, carry):
        for c in range(10):
            strip(s, 0, c, carry)
        with eng.Fori(0, (NST - 16) // 8) as j:
            for c in range(10, 18):
                strip(s, j, c, carry)
        for c in range(NST - 6, NST + 1):
            strip(s, 0, c, carry)

    sample(0, False)
    with eng.Fori(1, B) as s:
        sample(s, True)
    for c in range(lags):
        step(Tail(c), True)


XSTEPS = 3 + 2 * NCH
Z0 = 2 * NT
T0 = 2
V0 = 4
A0 = 4
S0 = 2
Y0 = 2


def sampled_layer(nc, m, src, dst):
    xs = src.rearrange("b c (k r) w -> (b c) k r w", r=TR)
    ys = dst.rearrange("b c (k r) w -> (b c) k r w", r=TR)
    z = nc.dram_tensor("sampled_rows", (B * STRIPS, 2, C, NT, W), F32, kind="Internal").ap()
    with ExitStack() as ctx:
        def sem(name):
            return ctx.enter_context(nc.semaphore(name))

        def sb(name, shape):
            return ctx.enter_context(nc.sbuf_tensor(name, shape, F32))

        xc = sb("x_chunks", [128, 2, FR, WP])
        xf = sb("x_first", [128, 4, WP])
        win = sb("windows", [128, 4, NT, WP])
        dif = sb("differences", [128, 2, 4, WP - 1])
        offx = sb("offsets_x", [128, 2, 2, W])
        offy = sb("offsets_y", [128, 5, 2, W])
        t1 = sb("term_left", [128, 3, 2, W])
        t3 = sb("terms", [128, 3, 2, W])
        smp = sb("samples", [128, 2, 2, W])
        win2 = sb("sample_windows", [128, 2, NT, WP])
        out = sb("out_rows", [128, 2, 2, W])
        cols = sb("sample_columns", [128, 2])
        moments = sb("moments", [128, 2])
        rows6 = sb("row_statistics", [128, TR, 6])

        t2 = m.kern[:].rearrange("p q k -> p (q k)").rearrange("p (a b w) -> p a b w", a=3, w=W)
        flat = m.stat_flat
        across = flat[:, 0:12 * W].rearrange("p (a b w) -> p a b w", a=6, w=W)
        down = flat[:, 12 * W:16 * W].rearrange("p (a b w) -> p a b w", a=2, w=W)
        weighed_rows = m.scratch[:, 16:16 + 4 * W].rearrange("p (a b w) -> p a b w", a=2, w=W)
        xr = [m.row_mean[:].rearrange("p a q -> p (a q)")[:, 0:2 * W].rearrange("p (a w) -> p a w", w=W),
              m.hidden_wide[:].rearrange("p a q -> p (a q)")[:, 0:2 * W].rearrange("p (a w) -> p a w", w=W)]

        ready = sem("buffers_ready")
        xf_loaded = sem("x_first_loaded")
        xc_loaded = [sem("x_chunk_loaded0"), sem("x_chunk_loaded1")]
        halo_loaded = sem("last_halo_loaded")
        win_loaded = [sem(f"window_loaded{k}") for k in range(4)]
        win_ready = sem("window_normalized")
        cols_ready = sem("sample_columns_ready")
        z_ready = sem("offset_sums")
        z_free = sem("offsets_copied")
        x_step = sem("x_step")
        mirrored = sem("last_row_mirrored")
        dif_ready = sem("differences_ready")
        terms_ready = sem("terms_ready")
        terms_added = sem("terms_added")
        across_ready = sem("across_ready")
        down_ready = sem("down_ready")
        weighed = sem("down_weighed")
        weighed_sum = sem("down_weighed_sum")
        edge = sem("edge_sampled")
        smp_ready = sem("samples_ready")
        smp_stored = [sem("samples_stored0"), sem("samples_stored1")]
        win2_loaded = [sem("sample_window0"), sem("sample_window1")]
        y_sums = sem("conv_sums")
        xr_loaded = [sem("residual_loaded0"), sem("residual_loaded1")]
        rows_ready = sem("rows_ready")
        stats_taken = sem("row_statistics_taken")
        moments_ready = sem("moments_ready")
        aggregated = sem("statistics_aggregated")
        stored = [sem("rows_stored0"), sem("rows_stored1")]
        block = ctx.enter_context(nc.Block())

        def window_slot(a):
            return {0: 2, NST: 3}.get(a.c, (a.c - 1) % 2)

        @block.sync
        def _(sp):
            sp.wait_ge(ready, 1)

            def store_samples(a):
                sp.wait_ge(smp_ready, a.g + 1 + S0)
                for b in range(NT):
                    sp.dma_start(z[ds(a.g, 1), :, :, b].rearrange("a r c w -> c (a r) w"),
                                 smp[C * b:C * b + C, a.c % 2]).then_inc(smp_stored[a.c % 2], 16)

            def store_rows(a):
                sp.wait_ge(rows_ready, a.n + Y0)
                for bl in range(2):
                    for r in range(2):
                        p0 = C * (2 * bl + r)
                        sp.dma_start(ys[ds(a.s * C, C), bl:NT:2, ds(a.i * 2 + (r - 2), 1)]
                                     .rearrange("c b r w -> c b (r w)"), out[p0:p0 + C, a.c % 2]) \
                            .then_inc(stored[a.c % 2], 16)

            def load_sample_window(a):
                sp.wait_ge(y_sums, a.n - 2 + Y0)
                if a.c == 1:
                    sp.wait_ge(smp_stored[0], a.s * (64 * (NST // 2 + 1)) + 64 + 16)
                n = NST // 2 + 1 - a.c % 2
                sp.wait_ge(smp_stored[a.c % 2], (a.s * n + a.half) * 64 + 64 + 16)
                sp.dma_start(win2[:, a.c % 2, :, 1:W + 1],
                             z[ds(a.g - 1, 2)].rearrange("a r c b w -> (a r c) b w")) \
                    .then_inc(win2_loaded[a.c % 2], 16)

            def load_residual(a):
                sp.wait_ge(rows_ready, a.n - 2 + Y0)
                for bl in range(2):
                    for r in range(2):
                        p0 = C * (2 * bl + r)
                        sp.dma_start(xr[a.c % 2][p0:p0 + C], xs[ds(a.s * C, C), bl:NT:2, ds(a.i * 2 + (r - 2), 1)]
                                     .rearrange("c b r w -> c b (r w)")).then_inc(xr_loaded[a.c % 2], 16)

            def load_window(a):
                sp.wait_ge(z_ready, (a.g - 1) * NT + Z0)
                slot = window_slot(a)
                for j in range(4):
                    b0, b1, d0, r = 0, NT, 0, j - 2
                    if a.c == 0 and j < 2:
                        b1, d0, r = NT - 1, 1, TR - 2 + j
                    if a.c == NST:
                        b0, r = (0, TR - 2 + j) if j < 2 else (1, j - 2)
                    rows = xs[ds(a.s * C, C), b0:b1, r] if a.c in (0, NST) else \
                        xs[ds(a.s * C, C), :, ds(a.i * 2 + r, 1)].rearrange("c b r w -> c b (r w)")
                    sp.dma_start(win[C * j:C * j + C, slot, d0:d0 + b1 - b0, 1:W + 1], rows) \
                        .then_inc(win_loaded[slot], 16)

            def load_first(s):
                if not isinstance(s, int):
                    sp.wait_ge(across_ready, s * STRIPS + (A0 - CS))
                for b in range(NT):
                    p0 = C * b
                    sp.dma_start(xf[p0:p0 + C, 2:4, 1:W + 1], xs[ds(s * C, C), b, 0:2]).then_inc(xf_loaded, 16)
                    if b > 0:
                        sp.dma_start(xf[p0:p0 + C, 0:2, 1:W + 1], xs[ds(s * C, C), b - 1, TR - 2:TR]) \
                            .then_inc(xf_loaded, 16)
                for b in range(NT):
                    sp.dma_start(xc[C * b:C * b + C, 0, :, 1:W + 1], xs[ds(s * C, C), b, 0:FR]) \
                        .then_inc(xc_loaded[0], 16)

            def step(a, carry):
                smp6, row9, res6 = before(a, 6, carry), before(a, 9, carry), before(a, 6, carry)
                if smp6:
                    store_samples(smp6)
                if row9 and row9.c:
                    store_rows(row9)
                if smp6 and smp6.c:
                    load_sample_window(smp6)
                if res6 and res6.c:
                    load_residual(res6)
                if a.s is END:
                    return
                load_window(a)
                if a.c == 0:
                    load_first(a.s)

            stream(sp, step, 9)
            for k in range(2):
                sp.wait_ge(stored[k], 64 * B * NST // 2 + 16)

        @block.scalar
        def _(act):
            act.wait_ge(ready, 1)

            def normalize(a):
                slot = window_slot(a)
                uses = {0: a.s * (NST // 2), 1: a.s * (NST // 2 - 1)}
                act.wait_ge(win_loaded[slot], (uses[slot] + a.use if slot < 2 else a.s) * 64 + 64)
                for j0, j1 in ((0, 2), (2, 4)) if slot > 1 else ((0, 4),):
                    b0 = 1 if a.c == 0 and j0 == 0 else 0
                    b1 = NT - 1 if a.c == NST and j0 == 2 else NT
                    v = win[C * j0:C * j1, slot, b0:b1, 1:W + 1]
                    ins = nc.scalar.activation(v, v, ACT.Identity, bias=cols[C * j0:C * j1, 0:1],
                                               scale=cols[C * j0:C * j1, 1:2])
                ins.then_inc(win_ready, 1)

            def load_chunk(a):
                act.wait_ge(across_ready, a.g + (2 - CS + A0))
                odd = 1 - a.odd
                for b in range(NT):
                    p0 = C * b
                    if a.c == NST - CS - 1:
                        act.dma_start(xc[p0:p0 + C, odd, 0:FR - 2, 1:W + 1], xs[ds(a.s * C, C), b, TR - FR + 2:TR]) \
                            .then_inc(xc_loaded[odd], 16)
                        if b < NT - 1:
                            act.dma_start(xc[p0:p0 + C, odd, FR - 2:FR, 1:W + 1], xs[ds(a.s * C, C), b + 1, 0:2]) \
                                .then_inc(halo_loaded, 16)
                    else:
                        act.dma_start(xc[p0:p0 + C, odd, :, 1:W + 1],
                                     xs[ds(a.s * C, C), b, ds(a.k * (2 * CS) + 2 * CS, FR)]).then_inc(xc_loaded[odd], 16)

            def normalize_rows(s, x, step):
                nc.scalar.activation(x[:, :, 1:W + 1], x[:, :, 1:W + 1], ACT.Identity, bias=cols[:, 0:1],
                                     scale=cols[:, 1:2]).then_inc(x_step, 1)
                act.wait_ge(x_step, s * XSTEPS + step)
                nc.scalar.copy(x[:, :, 0:WP:WP - 1], x[:, :, 2:WP - 2:WP - 5]).then_inc(x_step, 1)

            def normalize_first(s):
                act.wait_ge(xf_loaded, s * 112 + 112)
                normalize_rows(s, xf[:], 1)
                act.wait_ge(x_step, s * XSTEPS + 2)
                nc.scalar.copy(xf[0:C, 1, :], xf[0:C, 3, :]).then_inc(x_step, 1)

            def normalize_chunk0(s):
                act.wait_ge(xc_loaded[0], s * (64 * NCH // 2) + 64)
                normalize_rows(s, xc[:, 0], 4)

            def normalize_next(a):
                odd = 1 - a.odd
                half = a.j + ((a.c - 1) // CS + 1) // 2
                act.wait_ge(xc_loaded[odd], (a.s * (NCH // 2) + half) * 64 + 64)
                if a.c == NST - CS:
                    act.wait_ge(halo_loaded, a.s * 48 + 48)
                normalize_rows(a.s, xc[:, odd], a.k * 2 + 6)
                if a.c == NST - CS:
                    act.wait_ge(x_step, a.s * XSTEPS + a.k * 2 + 7)
                    p0 = C * (NT - 1)
                    nc.scalar.copy(xc[p0:, odd, FR - 2, :], xc[p0:, odd, FR - 4, :]).then_inc(mirrored, 1)

            def tanh(a):
                act.wait_ge(terms_ready, a.g - 2 + 1 + T0 + (a.c == 0))
                act.wait_ge(weighed, a.g - 4 + 1 + V0)
                dst = (offx[:, a.c % 2], offy[:, a.c % 4 if a.c else 4])
                for b in range(NT):
                    act.wait_ge(z_ready, a.g * NT + b + 1 + Z0)
                    for xy in range(2):
                        for r in range(2):
                            p0 = C * (2 * xy + r)
                            ins = nc.scalar.activation(dst[xy][C * b:C * b + C, r, :],
                                                       m.ps[p0:p0 + C, b, 0:W], ACT.Tanh,
                                                       bias=m.half_b_off[p0:p0 + C, 0:1], scale=0.5)
                    ins.then_inc(z_free, 1)

            def step(a, carry):
                if a.c == 0 and a.s is not END:
                    if carry:
                        act.wait_ge(win_ready, a.g + 1)
                        tanh(before(a, 1, carry))
                    for n, col in enumerate((m.shift_col, m.rstd_col)):
                        nc.scalar.copy(cols[:, n:n + 1], col[:, ds(a.s, 1)]).then_inc(cols_ready, 1)
                    act.wait_ge(cols_ready, a.s * 2 + 2)
                    normalize(a)
                    normalize_first(a.s)
                    return
                if a.s is not END:
                    if a.c % CS == CS - 1 and a.c < NST - CS:
                        load_chunk(a)
                    normalize(a)
                tanh(before(a, 1, carry))
                if a.s is not END:
                    if a.c == 1:
                        normalize_chunk0(a.s)
                    if a.c % CS == 0 and a.c < NST:
                        normalize_next(a)

            stream(act, step, 1)

        @block.tensor
        def _(pe):
            pe.wait_ge(ready, 1)

            def offset_conv(a):
                pe.wait_ge(win_ready, a.g + 2)
                for b in range(NT):
                    pe.wait_ge(z_free, a.g * NT + b + 1)
                    for dx in range(3):
                        ins = nc.tensor.matmul(m.ps[:, b, 0:W], m.w_off[:, dx, :],
                                               win[:, window_slot(a), b, dx:dx + W], start=(dx == 0), stop=(dx == 2))
                    ins.then_inc(z_ready, 1)

            def last_conv(a):
                pe.wait_ge(win2_loaded[a.c % 2], (a.s * (NST // 2) + a.use) * 16 + 16)
                pe.wait_ge(rows_ready, a.n - 2 + Y0)
                for bh in range(2):
                    for dx in range(3):
                        for bl in range(2):
                            ins = nc.tensor.matmul(m.ps[64 * bl:64 * bl + 64, 4 + 2 * (a.c % 2) + bh, 0:W],
                                                   m.w_dcn[:, dx, :],
                                                   win2[:, a.c % 2, 2 * bh + bl, dx:dx + W],
                                                   start=(dx == 0), stop=(dx == 2))
                ins.then_inc(y_sums, 1)

            def step(a, carry):
                if a.s is not END:
                    offset_conv(a)
                conv5 = before(a, 5, carry)
                if conv5 and conv5.c:
                    last_conv(conv5)

            stream(pe, step, 5)

        def rows_of(a):
            return xc[:, a.odd, 2 * a.t:2 * a.t + 4] if a.c else xf[:]

        @block.gpsimd
        def _(pool):
            pool.wait_ge(ready, 1)

            def differences(a):
                pool.wait_ge(x_step, a.s * XSTEPS + (a.k * 2 + 5 if a.c else 3))
                if a.c == NST - CS + 1:
                    pool.wait_ge(mirrored, a.s + 1)
                pool.wait_ge(terms_ready, a.g - 2 + 1 + T0 + (a.c == 0))
                x = rows_of(a)
                nc.gpsimd.tensor_tensor(dif[:, a.c % 2], x[:, :, 1:WP], x[:, :, 0:WP - 1], ALU.subtract) \
                    .then_inc(dif_ready, 1)

            def add_terms(a):
                pool.wait_ge(terms_ready, a.g + 1 + T0)
                pool.wait_ge(across_ready, a.g + A0)
                nc.gpsimd.tensor_tensor(t3[:], t1[:], t2[:], ALU.add).then_inc(terms_added, 1)

            def differences_down(a):
                pool.wait_ge(across_ready, a.g + 1 + A0)
                pool.wait_ge(weighed, a.g + V0)
                r = 3 * (a.c % 2)
                nc.gpsimd.tensor_tensor(down, across[:, r + 1:r + 3], across[:, r:r + 2], ALU.subtract) \
                    .then_inc(down_ready, 1)

            def step(a, carry):
                if a.s is not END:
                    differences(a)
                add1, down2 = before(a, 1, carry), before(a, 2, carry)
                if add1:
                    add_terms(add1)
                if down2:
                    differences_down(down2)

            stream(pool, step, 2)

        @block.vector
        def _(dve):
            nc.vector.memset(win2[:].rearrange("p a b c -> p (a b c)"), 0.0)
            nc.vector.memset(win[:].rearrange("p a b c -> p (a b c)"), 0.0)
            nc.vector.memset(xc[:].rearrange("p a b c -> p (a b c)"), 0.0)
            for k, (what, n) in enumerate(((win_ready, 1), (z_ready, Z0), (z_free, NT), (terms_ready, T0),
                                           (terms_added, 1), (across_ready, A0), (weighed, V0), (smp_ready, S0),
                                           (y_sums, Y0), (rows_ready, Y0), (stats_taken, Y0), (aggregated, 1),
                                           *((one, 16) for one in smp_stored + stored))):
                nc.vector.memset(m.scratch[:, k:k + 1], 0.0).then_inc(what, n)
            nc.vector.memset(xf[:].rearrange("p b c -> p (b c)"), 0.0).then_inc(ready, 1)
            dve.wait_ge(ready, 1)

            def terms(a):
                dve.wait_ge(z_free, a.g * NT + 2 * NT)
                dve.wait_ge(dif_ready, a.g + 1)
                dve.wait_ge(terms_added, a.g + 1)
                u, d = offx[:, a.c % 2], dif[:, a.c % 2]
                for r in range(3):
                    nc.vector.scalar_tensor_tensor(out=t1[:, r], in0=u, scalar=0.0, in1=d[:, r:r + 2, 0:W],
                                                   op0=ALU.max, op1=ALU.mult)
                    ins = nc.vector.scalar_tensor_tensor(out=t2[:, r], in0=u, scalar=0.0, in1=d[:, r:r + 2, 1:W + 1],
                                                         op0=ALU.min, op1=ALU.mult)
                ins.then_inc(terms_ready, 1)

            def sample_across(a):
                dve.wait_ge(terms_added, a.g + 2)
                dve.wait_ge(smp_ready, a.g - 2 + 1 + S0 + (a.c == 0))
                x = rows_of(a)
                for r in range(3):
                    ins = nc.vector.scalar_tensor_tensor(out=across[:, 3 * (a.c % 2) + r], in0=t3[:, r], scalar=-0.5,
                                                         in1=x[:, r:r + 2, 1:W + 1], op0=ALU.mult, op1=ALU.add)
                ins.then_inc(across_ready, 1)

            def weigh_down(a):
                dve.wait_ge(down_ready, a.g + 1)
                dve.wait_ge(smp_ready, a.g + S0)
                v = offy[:, a.c % 4 if a.c else 4]
                nc.vector.scalar_tensor_tensor(out=weighed_rows[:, 0], in0=v, scalar=0.0, in1=down[:, 0],
                                               op0=ALU.max, op1=ALU.mult)
                nc.vector.scalar_tensor_tensor(out=weighed_rows[:, 1], in0=v, scalar=0.0, in1=down[:, 1],
                                               op0=ALU.min, op1=ALU.mult).then_inc(weighed, 1)

            def add_down(a):
                dve.wait_ge(weighed, a.g + 1 + V0)
                nc.vector.tensor_tensor(weighed_rows[:, 0], weighed_rows[:, 0], weighed_rows[:, 1], ALU.add) \
                    .then_inc(weighed_sum, 1)

            def sample(a):
                dve.wait_ge(weighed_sum, a.g + 1)
                n = NST // 2 + 1 - a.c % 2
                dve.wait_ge(smp_stored[a.c % 2], (a.s * n + a.half) * 64 + 16)
                ins = nc.vector.scalar_tensor_tensor(out=smp[:, a.c % 2], in0=weighed_rows[:, 0], scalar=-0.5,
                                                     in1=across[:, 3 * (a.c % 2) + 1], op0=ALU.mult, op1=ALU.add)
                if a.c in (0, NST):
                    r, p0 = (0, 0) if a.c == 0 else (1, C * (NT - 1))
                    ins.then_inc(edge, 1)
                    dve.wait_ge(edge, a.s * 2 + (1 if a.c == 0 else 2))
                    ins = nc.vector.memset(smp[p0:p0 + C, 0, r], 0.0)
                ins.then_inc(smp_ready, 1)

            def residual(a):
                dve.wait_ge(y_sums, a.n + Y0)
                dve.wait_ge(xr_loaded[a.c % 2], (a.s * (NST // 2) + a.use) * 64 + 64)
                dve.wait_ge(stored[a.c % 2], (a.s * (NST // 2) + a.use) * 64 + 16)
                dve.wait_ge(stats_taken, a.n - 2 + Y0)
                y = m.ps[:, 4 + 2 * (a.c % 2):6 + 2 * (a.c % 2), 0:W]
                nc.vector.scalar_tensor_tensor(out=out[:, a.c % 2], in0=y, scalar=m.b_dcn[:, 0:1], in1=xr[a.c % 2],
                                               op0=ALU.add, op1=ALU.add).then_inc(rows_ready, 1)

            def statistics(a):
                dve.wait_ge(rows_ready, a.n + Y0)
                if a.c == 1:
                    dve.wait_ge(aggregated, a.s + 1)
                for h in range(2):
                    ins = nc.vector.bn_stats(
                        rows6[:, ds(a.i * 2 + (h - 2), 1)].rearrange("p a k -> p (a k)"), out[:, a.c % 2, h])
                ins.then_inc(stats_taken, 1)
                if a.c == NST:
                    dve.wait_ge(stats_taken, a.n + Y0)
                    nc.vector.memset(m.scratch[:, 15:16], 0.0)
                    nc.vector.bn_aggr(moments[:], rows6[:].rearrange("p r k -> p (r k)")).then_inc(moments_ready, 1)
                    dve.wait_ge(moments_ready, a.s + 1)
                    nc.vector.tensor_copy(m.agg[:, ds(a.s, 1)].rearrange("p a k -> p (a k)"), moments[:]) \
                        .then_inc(aggregated, 1)

            def step(a, carry):
                row5, down2, across1 = before(a, 5, carry), before(a, 2, carry), before(a, 1, carry)
                late = across1 and across1.c == 0
                if across1 and not late:
                    sample_across(across1)
                if a.s is not END:
                    terms(a)
                if down2:
                    weigh_down(down2)
                if row5 and row5.c:
                    residual(row5)
                if down2:
                    add_down(down2)
                if row5 and row5.c:
                    statistics(row5)
                if down2:
                    sample(down2)
                if late:
                    sample_across(across1)

            stream(dve, step, 5)


def program(nc, x, w1s, b1s, w2s, b2s, w_off, b_off, w_dcn, b_dcn, y):
    with ExitStack() as ctx:
        def sb(name, shape):
            return ctx.enter_context(nc.sbuf_tensor(name, shape, F32))

        m, w = Memory(), Memory()
        m.ps = ctx.enter_context(nc.psum_tensor("ps", [128, 8, 512], F32))
        statistics = sb("statistics", [128, NQ * NT * 6])
        m.stat = statistics[:].rearrange("p (q t k) -> p q t k", t=NT, k=6)
        m.stat_flat = statistics[:]
        m.agg = sb("sample_statistics", [128, B, 2])
        m.scratch = sb("scratch", [128, NQ * 2 * NT])
        m.kern = sb("kernels", [128, NQ, TAPS])
        m.ones = sb("ones", [128, 128])
        m.band = sb("band", [128, 3, TR])
        m.sel = sb("channel_select", [128, C])
        m.row_mask = sb("row_mask", [128, 3])
        m.row_mean = sb("row_mean", [128, 3, NQ])
        m.mean, m.rstd, m.chan_mean, m.chan_var, m.row_sum, m.col_sum = (
            sb(name, [128, NQ]) for name in ("mean", "rstd", "chan_mean", "chan_var", "row_sum", "col_sum"))
        m.pair, m.root, m.rough = (sb(name, [128, NQ // 2]) for name in ("pair", "root", "rough"))
        m.mean_col, m.rstd_col, m.shift_col, m.pooled, m.hidden = (
            sb(name, [128, B]) for name in
            ("mean_col", "rstd_col", "shift_col", "pooled", "hidden"))
        m.hidden_wide = sb("hidden_wide", [HID, B, 128])
        m.w_off = sb("w_off", [128, 3, 128])
        m.w_dcn = sb("w_dcn", [128, 3, 2 * C])
        m.half_b_off = sb("half_b_off", [128, 1])
        m.b_dcn = sb("b_dcn", [128, 1])
        w.loads = []
        nets = []
        for n in range(3):
            net = Memory()
            net.w1, net.b1 = sb(f"w1_{n}", [C, HID]), sb(f"b1_{n}", [HID, 1])
            net.w2, net.b2 = sb(f"w2_{n}", [HID, C * TAPS]), sb(f"b2_{n}", [128, C * TAPS])
            nets.append(net)
            w.loads += [(net.w1[:], w1s[n]), (net.b1[:], b1s[n].unsqueeze(1)), (net.w2[:], w2s[n]),
                        (net.b2[:], b2s[n].partition_broadcast(128))]
        for r in range(2):
            for dy in range(3):
                for dx in range(3):
                    p0 = C * (r + dy)
                    w.loads.append((m.w_off[p0:p0 + C, dx, :].rearrange("p (a r c) -> p a r c", a=2, r=2)[:, :, r],
                                    w_off[:, dy, dx]))
        for r in range(2):
            for dy in range(3):
                p0 = C * (r + dy)
                w.loads.append((m.w_dcn[p0:p0 + C, :, C * r:C * r + C], w_dcn[:, dy]))
        for a in range(2):
            for r in range(2):
                p0 = C * (2 * a + r)
                w.loads.append((m.half_b_off[p0:p0 + C], b_off[a].unsqueeze(1)))
        for b in range(4):
            w.loads.append((m.b_dcn[C * b:C * b + C], b_dcn.unsqueeze(1)))
        mid = [nc.dram_tensor(f"layer_{n}", (B, C, H, W), F32, kind="Internal").ap() for n in range(3)]

        setup(nc, m, w)
        input_statistics(nc, m, x)
        parameters(nc, m, 0, False, nets[0])
        depthwise(nc, m, 0, x, mid[0], True)
        parameters(nc, m, 1, False, nets[1])
        depthwise(nc, m, 1, mid[0], mid[1], True)
        parameters(nc, m, 2, False, None)
        sampled_layer(nc, m, mid[1], mid[2])
        parameters(nc, m, 3, True, nets[2])
        depthwise(nc, m, 3, mid[2], y, False)


def kernel(x, L0_conv_w1, L0_conv_b1, L0_conv_w2, L0_conv_b2, L1_conv_w1, L1_conv_b1, L1_conv_w2, L1_conv_b2,
           L2_conv_w_off, L2_conv_b_off, L2_conv_w_dcn, L2_conv_b_dcn,
           L3_conv_w1, L3_conv_b1, L3_conv_w2, L3_conv_b2):
    import numpy as np
    import concourse.bacc as bacc
    from concourse.bass_utils import run_bass_kernel_spmd

    nc = bacc.Bacc("TRN2", target_bir_lowering=False, num_devices=1)
    arrays = {}

    def inp(name, a):
        a = np.ascontiguousarray(a)
        arrays[name] = a
        return nc.dram_tensor(name, a.shape, mybir.dt.from_np(a.dtype), kind="ExternalInput").ap()

    ax = inp("x", x)
    w1s = [inp(f"w1_{n}_in", a) for n, a in enumerate((L0_conv_w1, L1_conv_w1, L3_conv_w1))]
    b1s = [inp(f"b1_{n}_in", a) for n, a in enumerate((L0_conv_b1, L1_conv_b1, L3_conv_b1))]
    w2s = [inp(f"w2_{n}_in", a) for n, a in enumerate((L0_conv_w2, L1_conv_w2, L3_conv_w2))]
    b2s = [inp(f"b2_{n}_in", a) for n, a in enumerate((L0_conv_b2, L1_conv_b2, L3_conv_b2))]
    w_off = inp("w_off_in", np.asarray(L2_conv_w_off).reshape(32, 2, 32, 3, 3).transpose(2, 3, 4, 1, 0))
    b_off = inp("b_off_in", np.asarray(L2_conv_b_off).reshape(32, 2).T)
    w_dcn = inp("w_dcn_in", np.asarray(L2_conv_w_dcn).transpose(1, 2, 3, 0))
    b_dcn = inp("b_dcn_in", L2_conv_b_dcn)
    y = nc.dram_tensor("y", (B, C, H, W), F32, kind="ExternalOutput").ap()
    program(nc, ax, w1s, b1s, w2s, b2s, w_off, b_off, w_dcn, b_dcn, y)
    r = run_bass_kernel_spmd(nc, [arrays], core_ids=[0])
    return r.results[0]["y"]
```
